# Optimizing a Trainium2 kernel written in Bass

```python
import numpy as np
import jax
import jax.numpy as jnp

def _softmax(x, axis=-1):
    return jax.nn.softmax(x, axis=axis)

def _gelu(x):
    return jax.nn.gelu(x, approximate=True)

def _silu(x):
    return jax.nn.silu(x)

def _sigmoid(x):
    return jax.nn.sigmoid(x)

def _layernorm(x, axis=-1, eps=1e-05):
    m = jnp.mean(x, axis=axis, keepdims=True)
    v = jnp.var(x, axis=axis, keepdims=True)
    return (x - m) / jnp.sqrt(v + eps)

def _scatter_add(tgt, idx, src, axis=0):
    return tgt.at[idx].add(src)

def _segment_sum(src, seg, n):
    return jax.ops.segment_sum(src, seg, n)
kernel_name = 'mk_gnn_resnorm_d2_gnn_r8_28f723'

def setup_inputs(seed: int=0):
    np.random.seed(seed)
    _w = jnp.asarray

    def _rec_inputs():
        import jax
        import jax.numpy as jnp
        _gk = jax.random.key(seed)
        x = -0.000202 + 1 * jax.random.normal(jax.random.fold_in(_gk, 1), (6250, 128), jnp.float32)
        src = jax.random.randint(jax.random.fold_in(_gk, 2), (100000,), 0, 6250, jnp.int32)
        dst = jnp.minimum((6250 * jax.random.uniform(jax.random.fold_in(_gk, 3), (100000,)) ** 2.0).astype(jnp.int32), 49999)
        _o = jnp.argsort(dst, stable=True)
        src = src[_o]
        dst = dst[_o]
        edge_weight = jax.random.uniform(jax.random.fold_in(_gk, 12), (100000,), jnp.float32, 0.0, 0.999999)
        return (x, src, dst, edge_weight)
    x, src, dst, edge_weight = _rec_inputs()

    def _L0_gnn_setup():
        import jax, jax.numpy as jnp
        import numpy as np
        N_NODES = 6250
        N_EDGES = 100000
        D_IN = 128
        U = 128
        H = 128
        key = jax.random.key(seed)
        ks = jax.random.split(key, 8)
        s = lambda d: 1.0 / np.sqrt(d)
        x = jax.random.normal(ks[0], (N_NODES, D_IN), dtype=jnp.float32)
        edge_index = jax.random.randint(ks[1], (2, N_EDGES), 0, N_NODES, dtype=jnp.int64)
        W1 = jax.random.normal(ks[2], (D_IN, U), dtype=jnp.float32) * s(D_IN)
        b1 = jax.random.normal(ks[3], (U,), dtype=jnp.float32) * 0.01
        W2 = jax.random.normal(ks[4], (2 * U, H), dtype=jnp.float32) * s(2 * U)
        b2 = jax.random.normal(ks[5], (H,), dtype=jnp.float32) * 0.01
        W3 = jax.random.normal(ks[6], (H, H), dtype=jnp.float32) * s(H)
        b3 = jax.random.normal(ks[7], (H,), dtype=jnp.float32) * 0.01
        return {'x': x, 'edge_index': edge_index, 'W1': W1, 'b1': b1, 'W2': W2, 'b2': b2, 'W3': W3, 'b3': b3}
    _L0_gnn_all = _L0_gnn_setup()
    _L0_gnn_in = {k: v for k, v in _L0_gnn_all.items() if k in ('W1', 'b1', 'W2', 'b2', 'W3', 'b3')}
    del _L0_gnn_all

    def _L1_gnn_setup():
        import jax, jax.numpy as jnp
        import numpy as np
        N_NODES = 12500
        N_EDGES = 200000
        D_IN = 128
        D_OUT = 128
        key = jax.random.key(seed)
        k1, k2, k3, k4 = jax.random.split(key, 4)
        X = jax.random.normal(k1, (N_NODES, D_IN), dtype=jnp.float32)
        edge_index = jax.random.randint(k2, (2, N_EDGES), 0, N_NODES, dtype=jnp.int32)
        edge_values = jax.random.uniform(k3, (N_EDGES,), dtype=jnp.float32)
        W = jax.random.normal(k4, (D_OUT, D_IN), dtype=jnp.float32) * 0.01
        b = jnp.zeros((D_OUT,), dtype=jnp.float32)
        return {'X': X, 'edge_index': edge_index, 'edge_values': edge_values, 'W': W, 'b': b}
    _L1_gnn_all = _L1_gnn_setup()
    _L1_gnn_in = {k: v for k, v in _L1_gnn_all.items() if k in ('W', 'b')}
    del _L1_gnn_all
    return {'x': x, 'src': src, 'dst': dst, 'edge_weight': edge_weight, 'L0_gnn_W1': _L0_gnn_in['W1'], 'L0_gnn_b1': _L0_gnn_in['b1'], 'L0_gnn_W2': _L0_gnn_in['W2'], 'L0_gnn_b2': _L0_gnn_in['b2'], 'L0_gnn_W3': _L0_gnn_in['W3'], 'L0_gnn_b3': _L0_gnn_in['b3'], 'L1_gnn_W': _L1_gnn_in['W'], 'L1_gnn_b': _L1_gnn_in['b']}

def reference(x, src, dst, edge_weight, L0_gnn_W1, L0_gnn_b1, L0_gnn_W2, L0_gnn_b2, L0_gnn_W3, L0_gnn_b3, L1_gnn_W, L1_gnn_b):
    import jax
    import jax.numpy as jnp

    def _L0_gnn_ref(x, edge_index, W1, b1, W2, b2, W3, b3):
        import jax, jax.numpy as jnp
        import numpy as np
        N_NODES = 6250
        N_EDGES = 100000
        D_IN = 128
        U = 128
        H = 128
        h = x @ W1 + b1
        src = edge_index[0]
        dst = edge_index[1]
        h_i = h[dst]
        h_j = h[src]
        e = jnp.concatenate([h_i, h_j - h_i], axis=-1)
        m = jax.nn.relu(e @ W2 + b2)
        m = jax.nn.relu(m @ W3 + b3)
        out = jax.ops.segment_max(m, dst, num_segments=N_NODES)
        return jax.nn.relu(out)

    def _L1_gnn_ref(X, edge_index, edge_values, W, b):
        import jax, jax.numpy as jnp
        import numpy as np
        N_NODES = 12500
        N_EDGES = 200000
        D_IN = 128
        D_OUT = 128
        dst = edge_index[0]
        src = edge_index[1]
        msgs = edge_values[:, None] * X[src]
        AX = jax.ops.segment_sum(msgs, dst, num_segments=X.shape[0])
        return jnp.einsum('nd,od->no', AX, W) + b
    edge_index = jnp.stack([src, dst])
    x = _layernorm(x + _L0_gnn_ref(x, edge_index, L0_gnn_W1, L0_gnn_b1, L0_gnn_W2, L0_gnn_b2, L0_gnn_W3, L0_gnn_b3), axis=-1)
    x = _layernorm(x + _L1_gnn_ref(x, edge_index, edge_weight, L1_gnn_W, L1_gnn_b), axis=-1)
    return x

_drawn_inputs = setup_inputs


def setup_inputs(seed=0):
    import zlib

    import numpy as np

    out = dict(_drawn_inputs(seed))
    spreads = {'L1_gnn_b': (0.0, 0.1)}
    factors = {'L0_gnn_b1': 8.0, 'L0_gnn_b2': 8.0, 'L0_gnn_b3': 5.819}
    for name, (base, spread) in spreads.items():
        noise = np.random.default_rng([zlib.crc32(name.encode()), seed]).standard_normal(out[name].shape)
        drawn = base * np.exp(spread * noise) if base else spread * noise
        out[name] = jnp.asarray(drawn.astype(out[name].dtype))
    for name, factor in factors.items():
        out[name] = (out[name] * factor).astype(out[name].dtype)
    return out
```

```python
import concourse.bass as bass
from concourse import mybir
from contextlib import ExitStack

P = 128
D = 128
N = 6250
E = 100000
H = -(-N // P)
NP = P * H
HX = -(-H // 4) * 4
GT = 4
GE = GT * P
TA = 2 * GT
PA = 98
T = PA * TA
EP = T * P
G = T // GT
UN = 4
IT = G // UN
EPA = TA * P
LASTN = N - (P - 1) * H
LASTE = E - (PA - 1) * EPA
CH = 7
CROWS = NP + P
NACC = GT
ZP = 5
EPS = 1e-5
assert H == CH * CH and G % UN == 0 and 0 < LASTE <= EPA and 0 < LASTN <= H

ALU = mybir.AluOpType
ACT = mybir.ActivationFunctionType
AX_X = mybir.AxisListType.X
F32 = mybir.dt.float32
I32 = mybir.dt.int32
U8 = mybir.dt.uint8
U16 = mybir.dt.uint16


def gnn_kernel(nc, x, src, dst, edge_weight, W1, b1, W2, b2, W3, b3, WL, bL, out):
    ds = bass.ds
    IOA = bass.IndirectOffsetOnAxis
    with ExitStack() as ctx:
        def sb(name, shape, dt=F32):
            return ctx.enter_context(nc.sbuf_tensor(name, shape, dt))

        def psum(name, shape):
            return ctx.enter_context(nc.psum_tensor(name, shape, F32))

        def sem(name):
            return ctx.enter_context(nc.semaphore(name))

        def dram(name, shape, dt=F32):
            return nc.dram_tensor(name, shape, dt, kind="Internal").ap()

        q_tab = dram("q_tab", [NP, D])
        c_tab = dram("c_tab", [CROWS + NP, D])
        seg_tab = dram("seg_tab", [EP, D])
        acc_tab = [dram(f"acc_tab{k}", [CROWS, D]) for k in range(NACC)]
        dst_tab = dram("dst_tab", [T, P])
        last_tab = dram("last_tab", [1, T])
        base_tab = dram("base_tab", [1, T], I32)
        seg_row_tab = dram("seg_row_tab", [G, 2, GE], U8)
        src_row_tab = dram("src_row_tab", [G, GE], U16)

        ident = sb("ident", [P, P])
        before = sb("before", [P, P])
        after = sb("after", [P, P])
        shift = sb("shift", [P, P])
        iota_p = sb("iota_p", [P, 1])
        iota_f = sb("iota_f", [P, P])
        node_id = sb("node_id", [P, H])
        spare = sb("spare", [P, H])
        trash = sb("trash", [P, 1])
        zeros = sb("zeros", [P, CROWS * D // P // ZP])

        w1 = sb("w1", [P, D])
        w2 = sb("w2", [P, 2, D])
        wpq = sb("wpq", [P, 2, D])
        w3 = sb("w3", [P, D])
        wl = sb("wl", [P, D])
        wlT = sb("wlT", [P, D])
        bias = sb("bias", [P, 3])
        bl_bc = sb("bl_bc", [P, D])

        dst_i = sb("dst_i", [PA, EPA], I32)
        src_i = sb("src_i", [PA, EPA], I32)
        w_a = sb("w_a", [PA, EPA])
        dst_f = sb("dst_f", [PA, EPA])
        src_f = sb("src_f", [PA, EPA])
        prev_i = sb("prev_i", [PA, 1], I32)
        prev_f = sb("prev_f", [PA, 1])
        cont = sb("cont", [PA, EPA])
        cid = sb("cid", [PA, EPA])
        cid_off = sb("cid_off", [PA, 1])
        base_f = sb("base_f", [PA, TA])
        base_i = sb("base_i", [PA, TA], I32)
        rel = sb("rel", [PA, EPA])
        opens = rel
        rel_u8 = sb("rel_u8", [PA, EPA], U8)
        cont_u8 = sb("cont_u8", [PA, EPA], U8)
        src_u16 = sb("src_u16", [PA, EPA], U16)
        base_row = sb("base_row", [1, T], I32)
        last_bc = sb("last_bc", [P, T])
        src_t = sb("src_t", [P, T])
        src_ti = sb("src_ti", [P, T + 2 * GT], I32)
        rel_t = sb("rel_t", [P, T])
        w_t = sb("w_t", [P, T])
        to_trash = sb("to_trash", [P, T])

        x_sb = sb("x_sb", [P, HX, D])
        p_sb = sb("p_sb", [P, HX, D])
        q_sb = sb("q_sb", [P, HX, D])
        rows = q_sb
        x1 = p_sb
        tile_of = sb("tile_of", [P, H])
        tile_i = sb("tile_i", [P, H], I32)
        start = sb("start", [P, H])
        end = sb("end", [P, H])
        full = sb("full", [P, H])
        seg = sb("seg", [P, H])
        seg_off = sb("seg_off", [P, 1])
        crow_i = sb("crow_i", [P, H], I32)
        end_i = sb("end_i", [P, H], I32)
        tmp_h = sb("tmp_h", [P, H])
        tmp_t = sb("tmp_t", [P, T])
        xT = sb("xT", [P, GE])
        hT = sb("hT", [P, GE])
        sq = sb("sq", [P, CH, D])
        stat = sb("stat", [P, 4, H])
        eps = sb("eps", [P, 1])

        src_idx = sb("src_idx", [P, UN, GT], I32)
        row_bc = sb("row_bc", [P, UN, 2 * GE], U8)
        win = sb("win", [P, 2, GT, D])
        qg = sb("qg", [P, UN, GT, D])
        oh = sb("oh", [P, 2, GE])
        junk = sb("junk", [P, GT, P])
        dup = sb("dup", [P, GT])
        move = sb("move", [P, GT])
        m1 = sb("m1", [P, 2, GE])
        m2 = sb("m2", [P, 2, GE])
        run = sb("run", [P, 2, GE])
        run_e = sb("run_e", [P, UN, GT, D])
        sel = m2
        msg = run_e
        axT = sb("axT", [P, CH, D])
        acc_sb = [x_sb, q_sb]

        m1_ps = psum("m1_ps", [P, 2, GE])
        z_ps = psum("z_ps", [P, 2, GE])
        t_ps = psum("t_ps", [P, 2, GE])
        s_ps = psum("s_ps", [P, 2, GE])
        by_col = lambda a: a[:, :, :].rearrange("p a (b d) -> p (a b) d", d=D)
        ax_ps = [by_col(m1_ps), by_col(t_ps)]
        yy_ps = [by_col(z_ps), by_col(s_ps)]

        pads_set = sem("pads_set")
        dst_ld, src_ld, w_ld, x_ld, wt_ld = map(sem, ("dst_ld", "src_ld", "w_ld", "x_ld", "wt_ld"))
        zeros_set, c_zero, acc_zero = map(sem, ("zeros_set", "c_zero", "acc_zero"))
        consts_a, consts = sem("consts_a"), sem("consts")
        dve_own, counted = sem("dve_own"), sem("counted")
        pool_waited, sp_waited = sem("pool_waited"), sem("sp_waited")
        opens_done, cid_sum = sem("opens_done"), sem("cid_sum")
        tabs_ready, dst_st, tabs_st = sem("tabs_ready"), sem("dst_st"), sem("tabs_st")
        back_ld, base_ld = sem("back_ld"), sem("base_ld")
        tr_in, tr_out, tr_copied = sem("tr_in"), sem("tr_out"), sem("tr_copied")
        wpq_done, x_cols = sem("wpq_done"), sem("x_cols")
        xT_ps, xT_sb, hT_ps, hT_sb, pq_ps, pq_sb = map(sem, ("xT_ps", "xT_sb", "hT_ps", "hT_sb", "pq_ps", "pq_sb"))
        q_st = sem("q_st")
        tile_found, tile_rows = sem("tile_found"), sem("tile_rows")
        start_done, start_next = sem("start_done"), sem("start_next")
        full_done, full_sum = sem("full_done"), sem("full_sum")
        node_rows, p_scat = sem("node_rows"), sem("p_scat")
        idx_done = sem("idx_done")
        row_ld = [sem(f"row_ld{s}") for s in range(UN)]
        win_ld = [sem(f"win_ld{s}") for s in range(2)]
        q_ld = [sem(f"q_ld{s}") for s in range(UN)]
        oh_done, m1_done, relu1, z_done, relu2, run_done, t_done, run_ev = map(
            sem, ("oh_done", "m1_done", "relu1", "z_done", "relu2", "run_done", "t_done", "run_ev"))
        run_st = [sem(f"run_st{s}") for s in range(UN)]
        dup_done, move_done = sem("dup_done"), sem("move_done")
        seg_ld = [sem(f"seg_ld{k}") for k in range(CH)]
        var_done, std_done, x1_done, x1_scat = map(sem, ("var_done", "std_done", "x1_done", "x1_scat"))
        row2_ld = [sem(f"row2_ld{s}") for s in range(2)]
        win2_ld = [sem(f"win2_ld{s}") for s in range(2)]
        sel_done, mt_done, mt_ev, msg_done, msg_ev = map(sem, ("sel_done", "mt_done", "mt_ev", "msg_done", "msg_ev"))
        acc_add = [sem(f"acc_add{k}") for k in range(NACC)]
        acc_ld = [sem(f"acc_ld{k}") for k in range(NACC)]
        axT_ps, axT_sb, y_ps, y_done = map(sem, ("axT_ps", "axT_sb", "y_ps", "y_done"))
        var2_done, std2_done, out_done, out_st = map(sem, ("var2_done", "std2_done", "out_done", "out_st"))

        def grp(i, r):
            return UN * i + r

        def uses(i, r):
            return 2 * i + r // 2 + 1

        def i_of(i, r):
            return i + r // UN

        def runs(i, r):
            return not isinstance(i, int) or 0 <= UN * i + r < G

        def old(i, r):
            return not isinstance(i, int) or UN * i + r >= 0

        node = lambda a: a.rearrange("(p h) d -> p h d", p=P)

        block = ctx.enter_context(nc.Block())

        @block.gpsimd
        def _(pool):
            nc.gpsimd.memset(zeros[:], 0.0).then_inc(zeros_set, 1)
            nc.gpsimd.memset(eps[:], EPS).then_inc(consts_a, 1)
            nc.gpsimd.memset(ident[:], 0.0).then_inc(consts_a, 1)
            nc.gpsimd.memset(before[:], 1.0).then_inc(consts_a, 1)
            nc.gpsimd.memset(after[:], 1.0).then_inc(consts_a, 1)
            nc.gpsimd.memset(shift[:], 0.0).then_inc(consts_a, 1)
            kw = dict(allow_small_or_imprecise_dtypes=True)
            nc.gpsimd.iota(iota_p[:], pattern=[[0, 1]], base=0, channel_multiplier=1, **kw).then_inc(consts, 1)
            nc.gpsimd.iota(iota_f[:], pattern=[[1, P]], base=0, channel_multiplier=0, **kw).then_inc(consts, 1)
            nc.gpsimd.iota(node_id[:], pattern=[[1, H]], base=0, channel_multiplier=H, **kw).then_inc(consts, 1)
            nc.gpsimd.iota(spare[:], pattern=[[1, H]], base=CROWS, channel_multiplier=H, **kw).then_inc(consts, 1)
            nc.gpsimd.iota(trash[:], pattern=[[0, 1]], base=NP, channel_multiplier=1, **kw).then_inc(consts, 1)
            pool.wait_ge(consts_a, 5)
            nc.gpsimd.affine_select(out=ident[:], in_=ident[:], compare_op=ALU.not_equal, fill=1.0, base=0,
                                    pattern=[[-1, P]], channel_multiplier=1).then_inc(consts, 1)
            nc.gpsimd.affine_select(out=before[:], in_=before[:], compare_op=ALU.is_gt, fill=0.0, base=0,
                                    pattern=[[-1, P]], channel_multiplier=1).then_inc(consts, 1)
            nc.gpsimd.affine_select(out=after[:], in_=after[:], compare_op=ALU.is_gt, fill=0.0, base=0,
                                    pattern=[[1, P]], channel_multiplier=-1).then_inc(consts, 1)
            nc.gpsimd.affine_select(out=shift[:], in_=shift[:], compare_op=ALU.not_equal, fill=1.0, base=-1,
                                    pattern=[[-1, P]], channel_multiplier=1).then_inc(consts, 1)

            pool.wait_ge(x_ld, 48)
            pool.wait_ge(pads_set, 6)
            nc.gpsimd.tensor_copy(qg[:, 0, :, :], x_sb[:, 0:GT, :]).then_inc(x_cols, 1)
            with pool.Fori(1, HX // GT) as g:
                pool.wait_ge(xT_ps, g)
                nc.gpsimd.tensor_copy(qg[:, 0, :, :], x_sb[:, ds(g * GT, GT), :]).then_inc(x_cols, 1)

            pool.wait_ge(tile_found, 1)
            pool.wait_ge(dst_st, 16)
            pool.wait_ge(q_st, 16)
            for h in range(H):
                pool.indirect_dma_start(rows[:, h, :], None, dst_tab[:, :], IOA(ap=tile_i[:, h:h + 1], axis=0)).then_inc(tile_rows, 16)
            pool.wait_ge(node_rows, 1)
            pool.wait_ge(pq_sb, 2 * (HX // GT))
            pool.wait_ge(c_zero, 16 * ZP)
            for h in range(H):
                pool.indirect_dma_start(c_tab[:, :], IOA(ap=crow_i[:, h:h + 1], axis=0), p_sb[:, h, :], None).then_inc(p_scat, 16)

            def gather(i, r):
                pool.wait_ge(idx_done, grp(i, r) + 1)
                if old(i, r - UN):
                    pool.wait_ge(m1_done, grp(i, r - UN) + 1)
                pool.sem_inc(pool_waited, 1)
                for j in range(GT):
                    pool.indirect_dma_start(qg[:, r, j, :], None, q_tab[:, :],
                                            IOA(ap=src_idx[:, r, j:j + 1], axis=0)).then_inc(q_ld[r], 16)

            for r in range(UN):
                gather(0, r)
            with pool.Fori(1, IT) as i:
                for r in range(UN):
                    gather(i, r)

            for s in range(UN):
                pool.wait_ge(run_st[s], 16 * IT)
            for h in range(H):
                pool.indirect_dma_start(rows[:, h, :], None, seg_tab[:, :],
                                        IOA(ap=end_i[:, h:h + 1], axis=0)).then_inc(seg_ld[h // CH], 16)
            for h in range(H):
                if h % CH == 0:
                    pool.wait_ge(x1_done, h // CH + 1)
                pool.indirect_dma_start(c_tab[:, :], IOA(ap=crow_i[:, h:h + 1], axis=0), x1[:, h, :], None).then_inc(x1_scat, 16)

            pool.wait_ge(acc_zero, 16 * ZP * NACC)

            def scatter(i, r):
                pool.wait_ge(idx_done, G + 2 + grp(i, r) + 1)
                pool.wait_ge(msg_ev, grp(i, r) + 1)
                for j in range(GT):
                    if old(i, r - 1):
                        pool.wait_ge(acc_add[j], 16 * grp(i, r))
                    pool.sem_inc(pool_waited, 1)
                    pool.indirect_dma_start(acc_tab[j][:, :], IOA(ap=src_idx[:, r, j:j + 1], axis=0), msg[:, r, j, :], None,
                                            compute_op=ALU.add).then_inc(acc_add[j], 16)

            for r in range(UN):
                scatter(0, r)
            with pool.Fori(1, IT) as i:
                for r in range(UN):
                    scatter(i, r)

        @block.sync
        def _(sp):
            ev = lambda a: a[0:(PA - 1) * EPA].rearrange("(p j) -> p j", j=EPA)
            tail = lambda a: a[(PA - 1) * EPA:E].rearrange("(a j) -> a j", a=1)
            cut = 96
            sp.wait_ge(pads_set, 4)
            for a, sbuf, s in ((dst, dst_i, dst_ld), (src, src_i, src_ld), (edge_weight, w_a, w_ld)):
                sp.dma_start(sbuf[0:cut, :], ev(a)[0:cut, :]).then_inc(s, 16)
                sp.dma_start(sbuf[cut:PA - 1, :], ev(a)[cut:PA - 1, :]).then_inc(s, 16)
                sp.dma_start(sbuf[PA - 1:PA, 0:LASTE], tail(a)).then_inc(s, 16)
                if a is dst:
                    sp.dma_start(prev_i[1:PA, :], ev(a)[:, EPA - 1:EPA], allow_slow_non_contiguous=True).then_inc(s, 16)
            sp.wait_ge(pads_set, 6)
            xv = x[0:(P - 1) * H, :].rearrange("(p h) d -> p h d", h=H)
            sp.dma_start(x_sb[0:112, 0:H, :], xv[0:112, :, :]).then_inc(x_ld, 16)
            sp.dma_start(x_sb[112:P - 1, 0:H, :], xv[112:P - 1, :, :]).then_inc(x_ld, 16)
            sp.dma_start(x_sb[P - 1:P, 0:LASTN, :], x[(P - 1) * H:N, :].rearrange("(a h) d -> a h d", a=1)).then_inc(x_ld, 16)

            sp.wait_ge(tabs_ready, 1)
            sp.dma_start(dst_tab.rearrange("(p k) e -> p (k e)", p=PA), dst_f[:, :]).then_inc(dst_st, 16)
            sp.dma_start(last_tab.rearrange("a (p k) -> p (a k)", p=PA),
                         dst_f[:, :].rearrange("p (k e) -> p k e", e=P)[:, :, P - 1], allow_slow_non_contiguous=True).then_inc(back_ld, 16)
            sp.wait_ge(back_ld, 16)
            sp.dma_start(last_bc[:, :], last_tab.to_broadcast([P, T])).then_inc(back_ld, 16)
            sp.wait_ge(tabs_ready, 2)
            sp.dma_start(base_tab.rearrange("a (p k) -> p (a k)", p=PA), base_i[:, :], allow_slow_non_contiguous=True).then_inc(base_ld, 16)
            for a, sbuf in ((seg_row_tab[:, 0, :], rel_u8), (seg_row_tab[:, 1, :], cont_u8), (src_row_tab, src_u16)):
                sp.dma_start(a.rearrange("(p q) e -> p q e", p=PA), sbuf[:, :].rearrange("p (q e) -> p q e", e=GE)).then_inc(tabs_st, 16)
            sp.wait_ge(base_ld, 16)
            sp.dma_start(base_row[:, :], base_tab[:, :]).then_inc(base_ld, 16)
            sp.wait_ge(pq_sb, 2 * (HX // GT))
            sp.dma_start(node(q_tab), q_sb[:, 0:H, :]).then_inc(q_st, 16)
            sp.wait_ge(tabs_st, 48)
            sp.wait_ge(base_ld, 32)
            sp.wait_ge(p_scat, 16 * H)

            def windows(i, r, sems):
                s = r % 2
                sp.sem_inc(sp_waited, 1)
                _, bases = nc.values_load_multi_w_load_instructions(
                    base_row[0:1, ds(GT * grp(i, r), GT)], engines=bass.OrderedEngineSet([mybir.EngineType.SP]), min_val=0, max_val=NP,
                    skip_runtime_bounds_check_because="a count of segments opened before a tile is below the count of nodes")
                for j, base in enumerate(bases):
                    sp.dma_start(win[:, s, j, :], c_tab[ds(base, P), :]).then_inc(sems[s], 16)

            def load0(i, r):
                if old(i, r - UN):
                    sp.wait_ge(run_done, grp(i, r - UN) + 1)
                    sp.sem_inc(sp_waited, 1)
                sp.dma_start(row_bc[:, r, :], seg_row_tab.rearrange("g a e -> g (a e)")[ds(grp(i, r), 1), :].to_broadcast([P, 2 * GE])).then_inc(row_ld[r], 16)
                if old(i, r - 2):
                    sp.wait_ge(m1_done, grp(i, r - 2) + 1)
                windows(i, r, win_ld)

            for r in range(UN):
                load0(0, r)
            with sp.Fori(1, IT) as i:
                for r in range(UN):
                    load0(i, r)

            sp.wait_ge(x1_scat, 16 * H)

            def load1(i, r):
                s = r % 2
                if old(i, r - 2):
                    sp.wait_ge(dup_done, grp(i, r - 2) + 1)
                    sp.wait_ge(msg_done, grp(i, r - 2) + 1)
                    sp.sem_inc(sp_waited, 1)
                sp.dma_start(row_bc[:, s, :].bitcast(U16), src_row_tab[ds(grp(i, r), 1), :].to_broadcast([P, GE])).then_inc(row2_ld[s], 16)
                windows(i, r, win2_ld)

            for r in range(UN):
                load1(0, r)
            with sp.Fori(1, IT) as i:
                for r in range(UN):
                    load1(i, r)

            for k in range(NACC):
                sp.wait_ge(acc_add[k], 16 * G)
            xv = out[0:(P - 1) * H, :].rearrange("(p h) d -> p h d", h=H)
            for c in range(CH):
                a, b = c * CH, (c + 1) * CH
                if c >= 2:
                    sp.wait_ge(axT_ps, c - 1)
                for k in range(NACC):
                    sp.dma_start(acc_sb[c % 2][:, k * CH:(k + 1) * CH, :], node(acc_tab[k][0:NP, :])[:, a:b, :]).then_inc(acc_ld[c % 2], 16)
            for c in range(CH):
                a, b = c * CH, (c + 1) * CH
                sp.wait_ge(out_done, c + 1)
                sp.dma_start(xv[0:112, a:b, :], x1[0:112, a:b, :]).then_inc(out_st, 16)
                sp.dma_start(xv[112:P - 1, a:b, :], x1[112:P - 1, a:b, :]).then_inc(out_st, 16)
                n = min(b, LASTN) - a
                if n > 0:
                    sp.dma_start(out[(P - 1) * H + a:(P - 1) * H + a + n, :].rearrange("(a h) d -> a h d", a=1),
                                 x1[P - 1:P, a:a + n, :]).then_inc(out_st, 16)
            sp.wait_ge(out_st, 16 * (2 * CH + -(-LASTN // CH)))

        @block.scalar
        def _(act):
            for sbuf, a in ((w1[:], W1), (w2[:], W2.rearrange("(k p) d -> p k d", p=P)), (w3[:], W3), (wl[:], WL),
                            (bias[:, 0:1], b1.rearrange("(p a) -> p a", a=1)), (bias[:, 1:2], b2.rearrange("(p a) -> p a", a=1)),
                            (bias[:, 2:3], b3.rearrange("(p a) -> p a", a=1)),
                            (bl_bc[:], bL.rearrange("(a d) -> a d", a=1).to_broadcast([P, D]))):
                act.dma_start(sbuf, a).then_inc(wt_ld, 16)
            act.wait_ge(zeros_set, 1)
            for tab, s in [(c_tab, c_zero)] + [(a, acc_zero) for a in acc_tab]:
                v = tab[0:CROWS, :].rearrange("(p a r) d -> a p (r d)", p=P, a=ZP)
                for a in range(ZP):
                    act.dma_start(v[a], zeros[:, :]).then_inc(s, 16)
            act.wait_ge(tr_out, 1)
            nc.scalar.activation(wlT[:], s_ps[:, 1, 0:D], ACT.Copy).then_inc(tr_copied, 1)

            act.wait_ge(wt_ld, 16 * 8)
            with act.Fori(0, HX // GT) as g:
                act.wait_ge(xT_ps, g + 1)
                nc.scalar.activation(xT[:], m1_ps[:, 0, :], ACT.Copy).then_inc(xT_sb, 1)
                act.wait_ge(hT_ps, g + 1)
                nc.scalar.activation(hT[:], z_ps[:, 0, :], ACT.Identity, bias=bias[:, 0:1]).then_inc(hT_sb, 1)
                act.wait_ge(pq_ps, g + 1)
                pq = t_ps[:, :, :].rearrange("p a (b f) -> p (a b) f", f=2 * D)
                nc.scalar.activation(p_sb[:, ds(g * GT, GT), :], pq[:, :, 0:D], ACT.Copy).then_inc(pq_sb, 1)
                nc.scalar.activation(q_sb[:, ds(g * GT, GT), :], pq[:, :, D:2 * D], ACT.Copy).then_inc(pq_sb, 1)

            def relu_1(i, r):
                s = r % 2
                act.wait_ge(m1_done, grp(i, r) + 1)
                if old(i, r - 2):
                    act.wait_ge(z_done, grp(i, r - 2) + 1)
                nc.scalar.activation(m1[:, s, :], m1_ps[:, s, :], ACT.Relu, bias=bias[:, 1:2]).then_inc(relu1, 1)

            def relu_2(i, r):
                s = r % 2
                act.wait_ge(z_done, grp(i, r) + 1)
                if old(i, r - 2):
                    act.wait_ge(run_done, grp(i, r - 2) + 1)
                nc.scalar.activation(m2[:, s, :], z_ps[:, s, :], ACT.Relu, bias=bias[:, 2:3]).then_inc(relu2, 1)

            def store(i, r):
                act.wait_ge(t_done, grp(i, r) + 1)
                if old(i, r - UN):
                    act.wait_ge(run_st[r % UN], 16 * i_of(i, r))
                nc.scalar.activation(run_e[:, r % UN, :, :], t_ps[:, r % 2, :].rearrange("p (t d) -> p t d", d=D), ACT.Copy).then_inc(run_ev, 1)
                act.wait_ge(run_ev, grp(i, r) + 1)
                act.dma_start(seg_tab.rearrange("(g t e) d -> g e t d", e=P, t=GT)[ds(grp(i, r), 1)].rearrange("a e t d -> (a e) t d"),
                              run_e[:, r % UN, :, :]).then_inc(run_st[r % UN], 16)

            def step0(i, r):
                for part, lag in ((relu_1, 0), (relu_2, 1), (store, 3)):
                    if runs(i, r - lag):
                        part(i, r - lag)

            for r in range(UN):
                step0(0, r)
            with act.Fori(1, IT) as i:
                for r in range(UN):
                    step0(i, r)
            for r in range(3):
                step0(IT, r)

            for c in range(CH):
                act.wait_ge(var_done, c + 1)
                cols = slice(c * CH, (c + 1) * CH)
                nc.scalar.activation(stat[:, 2, cols], stat[:, 1, cols], ACT.Sqrt, bias=eps[:], scale=1.0 / D).then_inc(std_done, 1)

            def mix_ev(i, r):
                s = r % 2
                act.wait_ge(mt_done, grp(i, r) + 1)
                if old(i, r - 2):
                    act.wait_ge(msg_done, grp(i, r - 2) + 1)
                nc.scalar.activation(m1[:, s, :], m1_ps[:, s, :], ACT.Copy).then_inc(mt_ev, 1)

            def message_ev(i, r):
                s = r % 2
                act.wait_ge(msg_done, grp(i, r) + 1)
                if old(i, r - UN):
                    for k in range(NACC):
                        act.wait_ge(acc_add[k], 16 * (grp(i, r - UN) + 1))
                nc.scalar.activation(msg[:, r % UN, :, :], z_ps[:, s, :].rearrange("p (t d) -> p t d", d=D), ACT.Copy).then_inc(msg_ev, 1)

            def step1(i, r):
                if runs(i, r):
                    mix_ev(i, r)
                if runs(i, r - 1):
                    message_ev(i, r - 1)

            for r in range(UN):
                step1(0, r)
            with act.Fori(1, IT) as i:
                for r in range(UN):
                    step1(i, r)
            step1(IT, 0)

            def root(c):
                act.wait_ge(var2_done, c + 1)
                cols = slice(c * CH, (c + 1) * CH)
                nc.scalar.activation(stat[:, 2, cols], stat[:, 1, cols], ACT.Sqrt, bias=eps[:], scale=1.0 / D).then_inc(std2_done, 1)

            for c in range(CH):
                act.wait_ge(axT_ps, c + 1)
                if c >= 1:
                    act.wait_ge(y_ps, c)
                nc.scalar.activation(axT[:, 0:CH, :], ax_ps[c % 2][:, 0:CH, :], ACT.Copy).then_inc(axT_sb, 1)
                if c >= 1:
                    root(c - 1)
            root(CH - 1)

        @block.vector
        def _(dve):
            chain = [0]

            def link(ins):
                chain[0] += 1
                ins.then_inc(dve_own, 1)
                dve.wait_ge(dve_own, chain[0])

            V = nc.vector
            V.memset(prev_i[:], -1).then_inc(pads_set, 1)
            V.memset(dst_i[:], N).then_inc(pads_set, 1)
            V.memset(src_i[:], N).then_inc(pads_set, 1)
            V.memset(w_a[:], 0.0).then_inc(pads_set, 1)
            V.memset(x_sb[:, H:HX, :], 0.0).then_inc(pads_set, 1)
            V.memset(x_sb[96:P, LASTN:H, :], 0.0).then_inc(pads_set, 1)
            link(V.memset(src_ti[:, T:], 0))

            dve.wait_ge(dst_ld, 64)
            V.tensor_copy(dst_f[:], dst_i[:]).then_inc(tabs_ready, 1)
            dve.wait_ge(tabs_ready, 1)
            link(V.tensor_copy(prev_f[:], prev_i[:]))
            V.tensor_tensor(cont[:, 1:], dst_f[:, 1:], dst_f[:, :EPA - 1], ALU.is_equal)
            link(V.tensor_tensor(cont[:, 0:1], dst_f[:, 0:1], prev_f[:], ALU.is_equal))
            V.tensor_copy(cont_u8[:], cont[:])
            link(V.tensor_scalar(opens[:], cont[:], -1.0, 1.0, ALU.mult, ALU.add))
            V.tensor_tensor_scan(cid[:], opens[:], opens[:], 0.0, ALU.add, ALU.max).then_inc(opens_done, 1)
            dve.wait_ge(src_ld, 48)
            V.tensor_copy(src_f[:], src_i[:]).then_inc(tr_in, 1)
            V.tensor_copy(src_u16[:], src_i[:])
            dve.wait_ge(wt_ld, 16 * 8)
            V.tensor_tensor(wpq[:, 0, :], w2[:, 0, :], w2[:, 1, :], ALU.subtract)
            V.tensor_copy(wpq[:, 1, :], w2[:, 1, :]).then_inc(wpq_done, 1)
            dve.wait_ge(cid_sum, 1)
            link(V.tensor_scalar(cid_off[:], s_ps[0:PA, 0, 0:1], -1.0, None, ALU.add))
            link(V.tensor_scalar(cid[:], cid[:], cid_off[:], None, ALU.add))
            cidv = cid[:, :].rearrange("p (k e) -> p k e", e=P)
            V.tensor_copy(base_i[:], cidv[:, :, 0])
            link(V.tensor_copy(base_f[:], cidv[:, :, 0]))
            link(V.tensor_tensor(rel[:, :].rearrange("p (k e) -> p k e", e=P), cidv,
                                 base_f[:, :].unsqueeze(2).to_broadcast([PA, TA, P]), ALU.subtract))
            V.tensor_copy(rel_u8[:], rel[:]).then_inc(tabs_ready, 1)
            V.tensor_copy(tmp_h[:, 0:1], iota_p[:]).then_inc(tr_in, 1)

            tv = lambda a: a.rearrange("p (q k) -> p k q", k=TA)
            pv = s_ps[:, :, :].rearrange("p a (b q) -> p (a b) q", q=P)[:, 0:TA, 0:PA]
            dve.wait_ge(tr_out, 2)
            V.tensor_copy(tv(src_t[:, :]), pv)
            link(V.tensor_copy(tv(src_ti[:, 0:T]), pv))
            V.tensor_scalar(to_trash[:], src_t[:], -1.0, trash[:], ALU.mult, ALU.add)
            V.tensor_copy(tmp_h[:, 0:1], iota_p[:]).then_inc(tr_copied, 1)
            dve.wait_ge(tr_out, 3)
            V.tensor_copy(tv(w_t[:, :]), pv).then_inc(tr_copied, 1)
            dve.wait_ge(tr_out, 4)
            V.tensor_copy(tv(rel_t[:, :]), pv).then_inc(tr_copied, 1)

            dve.wait_ge(back_ld, 32)
            dve.wait_ge(consts, 9)
            with dve.Fori(0, H) as h:
                V.tensor_scalar(tmp_t[:], last_bc[:], node_id[:, ds(h, 1)], None, ALU.is_lt, ALU.add,
                                accum_out=tile_of[:, ds(h, 1)]).then_inc(counted, 1)
                dve.wait_ge(counted, h + 1)
            link(V.tensor_scalar(tile_of[:], tile_of[:], float(T - 1), None, ALU.min))
            V.tensor_copy(tile_i[:], tile_of[:]).then_inc(tile_found, 1)
            dve.wait_ge(tile_rows, 16 * H)
            link(V.tensor_tensor(rows[:, 0:H, :], rows[:, 0:H, :], node_id[:, :].unsqueeze(2).to_broadcast([P, H, P]), ALU.is_lt))
            link(V.tensor_reduce(start[:], rows[:, 0:H, :], axis=AX_X, op=ALU.add))
            V.scalar_tensor_tensor(start[:], tile_of[:], float(P), start[:], ALU.mult, ALU.add).then_inc(start_done, 1)
            dve.wait_ge(start_next, 1)
            V.tensor_copy(end[:, 0:H - 1], start[:, 1:H])
            link(V.tensor_copy(end[:, H - 1:H], s_ps[:, 1, 0:1]))
            link(V.tensor_tensor(full[:], end[:], start[:], ALU.is_gt))
            V.tensor_tensor_scan(seg[:], full[:], full[:], 0.0, ALU.add, ALU.max).then_inc(full_done, 1)
            link(V.tensor_scalar(tmp_h[:], end[:], -1.0, 0.0, ALU.add, ALU.max))
            V.tensor_copy(end_i[:], tmp_h[:])
            dve.wait_ge(full_sum, 1)
            link(V.tensor_scalar(seg_off[:], s_ps[:, 1, 1:2], -1.0, None, ALU.add))
            link(V.scalar_tensor_tensor(seg[:], seg[:], seg_off[:], spare[:], ALU.add, ALU.subtract))
            link(V.tensor_tensor(seg[:], seg[:], full[:], ALU.mult))
            link(V.tensor_tensor(seg[:], seg[:], spare[:], ALU.add))
            V.tensor_copy(crow_i[:], seg[:]).then_inc(node_rows, 1)

            def indices(i, r):
                V.tensor_copy(src_idx[:, r % UN, :], src_ti[:, ds(GT * grp(i, r), GT)]).then_inc(idx_done, 1)

            def one_hot(i, r):
                s = r % 2
                dve.wait_ge(row_ld[r % UN], 16 * (i + 1))
                if old(i, r - 2):
                    dve.wait_ge(m1_done, grp(i, r - 2) + 1)
                V.tensor_scalar(oh[:, s, :], row_bc[:, r % UN, 0:GE], iota_p[:], None, ALU.is_equal).then_inc(oh_done, 1)

            def scan(i, r):
                s = r % 2
                dve.wait_ge(relu2, grp(i, r) + 1)
                if old(i, r - 2):
                    dve.wait_ge(t_done, grp(i, r - 2) + 1)
                first = 0.0
                if old(i, r - 1):
                    dve.wait_ge(run_done, grp(i, r))
                    first = run[:, 1 - s, GE - 1:GE]
                V.tensor_tensor_scan(run[:, s, :], row_bc[:, r % UN, GE:2 * GE], m2[:, s, :], first, ALU.mult, ALU.max).then_inc(run_done, 1)

            def step0(i, r):
                if runs(i, r):
                    if old(i, r - 2):
                        dve.wait_ge(q_ld[(r - 2) % UN], 16 * GT * (i_of(i, r - 2) + 1))
                    indices(i, r + 2)
                    one_hot(i, r)
                if runs(i, r - 2):
                    scan(i + (r - 2) // UN if isinstance(i, int) else i, (r - 2) % UN if isinstance(i, int) else r - 2)

            indices(0, 0)
            indices(0, 1)
            for r in range(UN):
                step0(0, r)
            with dve.Fori(1, IT) as i:
                for r in range(UN):
                    step0(i, r)
            for r in range(2):
                step0(IT, r)

            def normalise(c, var, std, done):
                cols = slice(c * CH, (c + 1) * CH)
                v = x1[:, cols, :]
                link(V.tensor_reduce(stat[:, 0, cols], v, axis=AX_X, op=ALU.add))
                link(V.tensor_scalar(stat[:, 0, cols], stat[:, 0, cols], -1.0 / D, None, ALU.mult))
                link(V.tensor_tensor(v, v, stat[:, 0, cols].unsqueeze(2).to_broadcast([P, CH, D]), ALU.add))
                link(V.tensor_tensor(sq[:], v, v, ALU.mult))
                V.tensor_reduce(stat[:, 1, cols], sq[:], axis=AX_X, op=ALU.add).then_inc(var, 1)
                dve.wait_ge(std, c + 1)
                link(V.reciprocal(stat[:, 3, cols], stat[:, 2, cols]))
                V.tensor_tensor(v, v, stat[:, 3, cols].unsqueeze(2).to_broadcast([P, CH, D]), ALU.mult).then_inc(done, 1)

            for c in range(CH):
                cols = slice(c * CH, (c + 1) * CH)
                dve.wait_ge(seg_ld[c], 16 * CH)
                link(V.tensor_tensor(rows[:, cols, :], rows[:, cols, :], full[:, cols].unsqueeze(2).to_broadcast([P, CH, D]), ALU.mult))
                link(V.tensor_tensor(x1[:, cols, :], rows[:, cols, :], x_sb[:, cols, :], ALU.add))
                normalise(c, var_done, std_done, x1_done)

            def selections(i, r):
                s = r % 2
                dve.wait_ge(row2_ld[s], 16 * uses(i, r))
                if old(i, r - 2):
                    dve.wait_ge(mt_done, grp(i, r - 2) + 1)
                V.tensor_tensor(oh[:, s, :].rearrange("p (t c) -> p t c", c=P), iota_f[:, :].unsqueeze(1).to_broadcast([P, GT, P]),
                                rel_t[:, ds(GT * grp(i, r), GT)].unsqueeze(2).to_broadcast([P, GT, P]), ALU.is_equal)
                src16 = row_bc[:, s, :].bitcast(U16)
                tile_src = lambda j: (src16[:, j * P:(j + 1) * P], src_t[:, ds(GT * grp(i, r) + j, 1)])
                for j in range(GT):
                    row, col = tile_src(j)
                    last = V.tensor_scalar(sel[:, s, j * P:(j + 1) * P], row, col, w_t[:, ds(GT * grp(i, r) + j, 1)], ALU.is_equal, ALU.mult)
                last.then_inc(sel_done, 1)
                if old(i, r - 1):
                    dve.wait_ge(idx_done, G + 2 + grp(i, r))
                for j in range(GT):
                    row, col = tile_src(j)
                    last = V.scalar_tensor_tensor(junk[:, j, :], row, col, before[:], ALU.is_equal, ALU.mult, accum_out=dup[:, j:j + 1])
                last.then_inc(dup_done, 1)

            def accumulator_rows(i, r):
                dve.wait_ge(dup_done, grp(i, r) + 1)
                V.scalar_tensor_tensor(move[:], dup[:], 0.5, to_trash[:, ds(GT * grp(i, r), GT)], ALU.is_gt, ALU.mult).then_inc(move_done, 1)
                if old(i, r - UN):
                    for k in range(NACC):
                        dve.wait_ge(acc_add[k], 16 * (grp(i, r - UN) + 1))
                dve.wait_ge(move_done, grp(i, r) + 1)
                V.tensor_tensor(src_idx[:, r, :], move[:], src_t[:, ds(GT * grp(i, r), GT)], ALU.add).then_inc(idx_done, 1)

            def step1(i, r):
                selections(i, r)
                accumulator_rows(i, r)

            for r in range(UN):
                step1(0, r)
            with dve.Fori(1, IT) as i:
                for r in range(UN):
                    step1(i, r)

            for c in range(CH):
                v = x1[:, c * CH:(c + 1) * CH, :]
                link(V.tensor_tensor(v, v, bl_bc[:, :].unsqueeze(1).to_broadcast([P, CH, D]), ALU.add))
                dve.wait_ge(y_ps, c + 1)
                ins = V.tensor_tensor(v, v, yy_ps[c % 2][:, 0:CH, :], ALU.add)
                ins.then_inc(y_done, 1)
                dve.wait_ge(y_done, c + 1)
                normalise(c, var2_done, std2_done, out_done)

        @block.tensor
        def _(pe):
            mm = nc.tensor.matmul
            pe.wait_ge(consts, 9)
            pe.wait_ge(wt_ld, 16 * 8)
            nc.tensor.transpose(s_ps[:, 1, 0:D], wl[:], ident[:]).then_inc(tr_out, 1)
            pe.wait_ge(opens_done, 1)
            mm(s_ps[0:PA, 0, 0:1], lhsT=after[0:PA, 0:PA], rhs=cid[:, EPA - 1:EPA], start=True, stop=True).then_inc(cid_sum, 1)

            def by_tile(a, n):
                for k in range(TA):
                    last = nc.tensor.transpose(s_ps[:, k // 4, (k % 4) * P:(k % 4) * P + PA], a[:, k * P:(k + 1) * P], ident[0:PA, 0:PA])
                last.then_inc(tr_out, 1)

            pe.wait_ge(tr_in, 2)
            pe.wait_ge(tr_copied, 1)
            by_tile(src_f, 1)
            pe.wait_ge(w_ld, 48)
            pe.wait_ge(tr_copied, 2)
            by_tile(w_a, 2)
            pe.wait_ge(tr_copied, 3)
            by_tile(rel, 3)

            pe.wait_ge(wpq_done, 1)
            pq = t_ps[:, :, :].rearrange("p a (b f) -> p (a b) f", f=2 * D)
            with pe.Fori(0, HX // GT) as g:
                pe.wait_ge(x_cols, g + 1)
                for j in range(GT):
                    last = nc.tensor.transpose(m1_ps[:, 0, j * P:(j + 1) * P], qg[:, 0, j, :], ident[:])
                last.then_inc(xT_ps, 1)
                pe.wait_ge(xT_sb, g + 1)
                mm(z_ps[:, 0, :], lhsT=w1[:], rhs=xT[:], start=True, stop=True).then_inc(hT_ps, 1)
                pe.wait_ge(hT_sb, g + 1)
                for j in range(GT):
                    last = mm(pq[:, j, :], lhsT=hT[:, j * P:(j + 1) * P], rhs=wpq[:, :, :].rearrange("p a d -> p (a d)"), start=True, stop=True)
                last.then_inc(pq_ps, 1)
                pe.wait_ge(pq_sb, 2 * g + 2)

            pe.wait_ge(start_done, 1)
            pe.wait_ge(tr_copied, 4)
            mm(s_ps[:, 1, 0:1], lhsT=shift[:], rhs=start[:, 0:1], start=True, stop=True).then_inc(start_next, 1)
            pe.wait_ge(full_done, 1)
            mm(s_ps[:, 1, 1:2], lhsT=after[:], rhs=seg[:, H - 1:H], start=True, stop=True).then_inc(full_sum, 1)

            def gathered(i, r):
                s = r % 2
                pe.wait_ge(q_ld[r], 16 * GT * (i + 1))
                pe.wait_ge(win_ld[s], 16 * GT * uses(i, r))
                pe.wait_ge(oh_done, grp(i, r) + 1)
                if old(i, r - 2):
                    pe.wait_ge(relu1, grp(i, r - 2) + 1)
                for j in range(GT):
                    c = slice(j * P, (j + 1) * P)
                    mm(m1_ps[:, s, c], lhsT=qg[:, r, j, :], rhs=ident[:], start=True, stop=False)
                    last = mm(m1_ps[:, s, c], lhsT=win[:, s, j, :], rhs=oh[:, s, c], start=False, stop=True)
                last.then_inc(m1_done, 1)

            def second(i, r):
                s = r % 2
                pe.wait_ge(relu1, grp(i, r) + 1)
                if old(i, r - 2):
                    pe.wait_ge(relu2, grp(i, r - 2) + 1)
                mm(z_ps[:, s, :], lhsT=w3[:], rhs=m1[:, s, :], start=True, stop=True).then_inc(z_done, 1)

            def by_edge(i, r):
                s = r % 2
                pe.wait_ge(run_done, grp(i, r) + 1)
                if old(i, r - 2):
                    pe.wait_ge(run_ev, grp(i, r - 2) + 1)
                for j in range(GT):
                    c = slice(j * P, (j + 1) * P)
                    last = nc.tensor.transpose(t_ps[:, s, c], run[:, s, c], ident[:])
                last.then_inc(t_done, 1)

            def step0(i, r):
                for part, lag in ((gathered, 0), (second, 1), (by_edge, 3)):
                    if runs(i, r - lag):
                        part(i, r - lag)

            for r in range(UN):
                step0(0, r)
            with pe.Fori(1, IT) as i:
                for r in range(UN):
                    step0(i, r)
            for r in range(3):
                step0(IT, r)

            def mix(i, r):
                s = r % 2
                pe.wait_ge(sel_done, grp(i, r) + 1)
                if old(i, r - 2):
                    pe.wait_ge(mt_ev, grp(i, r - 2) + 1)
                for j in range(GT):
                    c = slice(j * P, (j + 1) * P)
                    last = mm(m1_ps[:, s, c], lhsT=oh[:, s, c], rhs=sel[:, s, c], start=True, stop=True)
                last.then_inc(mt_done, 1)

            def message(i, r):
                s = r % 2
                pe.wait_ge(mt_ev, grp(i, r) + 1)
                pe.wait_ge(win2_ld[s], 16 * GT * uses(i, r))
                if old(i, r - 2):
                    pe.wait_ge(msg_ev, grp(i, r - 2) + 1)
                for j in range(GT):
                    c = slice(j * P, (j + 1) * P)
                    last = mm(z_ps[:, s, c], lhsT=m1[:, s, c], rhs=win[:, s, j, :], start=True, stop=True)
                last.then_inc(msg_done, 1)

            def step1(i, r):
                if runs(i, r):
                    mix(i, r)
                if runs(i, r - 1):
                    message(i, r - 1)

            for r in range(UN):
                step1(0, r)
            with pe.Fori(1, IT) as i:
                for r in range(UN):
                    step1(i, r)
            step1(IT, 0)

            for c in range(CH):
                pe.wait_ge(acc_ld[c % 2], 16 * NACC * (c // 2 + 1))
                if c >= 2:
                    pe.wait_ge(axT_sb, c - 1)
                for h in range(CH):
                    for k in range(NACC):
                        last = mm(ax_ps[c % 2][:, h, :], lhsT=acc_sb[c % 2][:, k * CH + h, :], rhs=ident[:],
                                  start=(k == 0), stop=(k == NACC - 1))
                last.then_inc(axT_ps, 1)
                pe.wait_ge(axT_sb, c + 1)
                if c >= 2:
                    pe.wait_ge(y_done, c - 1)
                for h in range(CH):
                    last = mm(yy_ps[c % 2][:, h, :], lhsT=axT[:, h, :], rhs=wlT[:], start=True, stop=True)
                last.then_inc(y_ps, 1)


_INS = ["x", "src", "dst", "edge_weight", "L0_gnn_W1", "L0_gnn_b1", "L0_gnn_W2", "L0_gnn_b2", "L0_gnn_W3", "L0_gnn_b3",
        "L1_gnn_W", "L1_gnn_b"]


def kernel(**inputs):
    import numpy as np
    import concourse.bacc as bacc
    from concourse.bass_utils import run_bass_kernel_spmd

    nc = bacc.Bacc("TRN2", target_bir_lowering=False, num_devices=1)
    arrays, args = {}, []
    for name in _INS:
        a = np.ascontiguousarray(inputs[name])
        arrays[f"in_{name}_dram"] = a
        args.append(nc.dram_tensor(f"in_{name}_dram", a.shape, mybir.dt.from_np(a.dtype), kind="ExternalInput").ap())
    out = nc.dram_tensor("out_dram", (N, D), F32, kind="ExternalOutput").ap()
    gnn_kernel(nc, *args, out)
    r = run_bass_kernel_spmd(nc, [arrays], core_ids=[0])
    return r.results[0]["out_dram"]
```

```python
import concourse.bass as bass
from concourse import mybir
from contextlib import ExitStack

P = 128
D = 128
N = 6250
E = 100000
H = -(-N // P)
NP = P * H
HX = -(-H // 4) * 4
GT = 4
GE = GT * P
TA = 2 * GT
PA = 98
T = PA * TA
EP = T * P
G = T // GT
UN = 4
IT = G // UN
EPA = TA * P
LASTN = N - (P - 1) * H
LASTE = E - (PA - 1) * EPA
CH = 7
CROWS = NP + P
NACC = GT
ZP = 5
EPS = 1e-5
assert H == CH * CH and G % UN == 0 and 0 < LASTE <= EPA and 0 < LASTN <= H

ALU = mybir.AluOpType
ACT = mybir.ActivationFunctionType
AX_X = mybir.AxisListType.X
F32 = mybir.dt.float32
I32 = mybir.dt.int32
U8 = mybir.dt.uint8
U16 = mybir.dt.uint16


def gnn_kernel(nc, x, src, dst, edge_weight, W1, b1, W2, b2, W3, b3, WL, bL, out):
    ds = bass.ds
    IOA = bass.IndirectOffsetOnAxis
    with ExitStack() as ctx:
        def sb(name, shape, dt=F32):
            return ctx.enter_context(nc.sbuf_tensor(name, shape, dt))

        def psum(name, shape):
            return ctx.enter_context(nc.psum_tensor(name, shape, F32))

        def sem(name):
            return ctx.enter_context(nc.semaphore(name))

        def dram(name, shape, dt=F32):
            return nc.dram_tensor(name, shape, dt, kind="Internal").ap()

        q_tab = dram("q_tab", [NP, D])
        c_tab = dram("c_tab", [CROWS + NP, D])
        seg_tab = dram("seg_tab", [EP, D])
        acc_tab = [dram(f"acc_tab{k}", [CROWS, D]) for k in range(NACC)]
        dst_tab = dram("dst_tab", [T, P])
        last_tab = dram("last_tab", [1, T])
        base_tab = dram("base_tab", [1, T], I32)
        seg_row_tab = dram("seg_row_tab", [G, 2, GE], U8)
        src_row_tab = dram("src_row_tab", [G, GE], U16)

        ident = sb("ident", [P, P])
        before = sb("before", [P, P])
        after = sb("after", [P, P])
        shift = sb("shift", [P, P])
        iota_p = sb("iota_p", [P, 1])
        iota_f = sb("iota_f", [P, P])
        node_id = sb("node_id", [P, H])
        spare = sb("spare", [P, H])
        trash = sb("trash", [P, 1])
        zeros = sb("zeros", [P, CROWS * D // P // ZP])

        w1 = sb("w1", [P, D])
        w2 = sb("w2", [P, 2, D])
        wpq = sb("wpq", [P, 2, D])
        w3 = sb("w3", [P, D])
        wl = sb("wl", [P, D])
        wlT = sb("wlT", [P, D])
        bias = sb("bias", [P, 3])
        bl_bc = sb("bl_bc", [P, D])

        dst_i = sb("dst_i", [PA, EPA], I32)
        src_i = sb("src_i", [PA, EPA], I32)
        w_a = sb("w_a", [PA, EPA])
        dst_f = sb("dst_f", [PA, EPA])
        src_f = sb("src_f", [PA, EPA])
        prev_i = sb("prev_i", [PA, 1], I32)
        prev_f = sb("prev_f", [PA, 1])
        cont = sb("cont", [PA, EPA])
        cid = sb("cid", [PA, EPA])
        cid_off = sb("cid_off", [PA, 1])
        base_f = sb("base_f", [PA, TA])
        base_i = sb("base_i", [PA, TA], I32)
        rel = sb("rel", [PA, EPA])
        opens = rel
        rel_u8 = sb("rel_u8", [PA, EPA], U8)
        cont_u8 = sb("cont_u8", [PA, EPA], U8)
        src_u16 = sb("src_u16", [PA, EPA], U16)
        base_row = sb("base_row", [1, T], I32)
        last_bc = sb("last_bc", [P, T])
        src_t = sb("src_t", [P, T])
        src_ti = sb("src_ti", [P, T + 2 * GT], I32)
        rel_t = sb("rel_t", [P, T])
        w_t = sb("w_t", [P, T])
        to_trash = sb("to_trash", [P, T])

        x_sb = sb("x_sb", [P, HX, D])
        p_sb = sb("p_sb", [P, HX, D])
        q_sb = sb("q_sb", [P, HX, D])
        rows = q_sb
        x1 = p_sb
        y = x_sb
        res = q_sb
        acc_sb = [x_sb, q_sb, p_sb]
        tile_of = sb("tile_of", [P, H])
        tile_i = sb("tile_i", [P, H], I32)
        start = sb("start", [P, H])
        end = sb("end", [P, H])
        full = sb("full", [P, H])
        seg = sb("seg", [P, H])
        seg_off = sb("seg_off", [P, 1])
        crow_i = sb("crow_i", [P, H], I32)
        end_i = sb("end_i", [P, H], I32)
        tmp_h = sb("tmp_h", [P, H])
        tmp_t = sb("tmp_t", [P, T])
        xT = sb("xT", [P, GE])
        hT = sb("hT", [P, GE])
        part = sb("part", [P, CH, 6])
        mv = sb("mv", [P, H, 2])
        std = sb("std", [P, H])
        rstd = sb("rstd", [P, H])
        eps = sb("eps", [P, 1])

        src_idx = sb("src_idx", [P, UN, GT], I32)
        row_bc = sb("row_bc", [P, UN, 2 * GE], U8)
        win = sb("win", [P, UN, GT, D])
        qg = sb("qg", [P, UN, GT, D])
        oh = sb("oh", [P, 2, GE])
        junk = sb("junk", [P, GT, P])
        dup = sb("dup", [P, GT])
        move = sb("move", [P, GT])
        m1 = sb("m1", [P, 2, GE])
        m2 = sb("m2", [P, 2, GE])
        run = sb("run", [P, 2, GE])
        run_e = sb("run_e", [P, UN, GT, D])
        sel = m2
        msg = run_e

        m1_ps = psum("m1_ps", [P, 2, GE])
        z_ps = psum("z_ps", [P, 2, GE])
        t_ps = psum("t_ps", [P, 2, GE])
        s_ps = psum("s_ps", [P, 2, GE])
        by_col = lambda a: a[:, :, :].rearrange("p a (b d) -> p (a b) d", d=D)
        x1T_ps = [by_col(m1_ps), by_col(t_ps)]
        y_ps = [by_col(z_ps), by_col(s_ps)]
        x1T = [by_col(m1), by_col(m2)]

        pads_set = sem("pads_set")
        dst_ld, src_ld, w_ld, x_ld, wt_ld = map(sem, ("dst_ld", "src_ld", "w_ld", "x_ld", "wt_ld"))
        zeros_set, c_zero, acc_zero = map(sem, ("zeros_set", "c_zero", "acc_zero"))
        consts_a, consts = sem("consts_a"), sem("consts")
        dve_own, counted = sem("dve_own"), sem("counted")
        pool_waited, sp_waited = sem("pool_waited"), sem("sp_waited")
        opens_done, cid_sum = sem("opens_done"), sem("cid_sum")
        tabs_ready, dst_st, tabs_st = sem("tabs_ready"), sem("dst_st"), sem("tabs_st")
        back_ld, base_ld = sem("back_ld"), sem("base_ld")
        tr_in, tr_out, tr_copied = sem("tr_in"), sem("tr_out"), sem("tr_copied")
        wpq_done, x_cols = sem("wpq_done"), sem("x_cols")
        xT_ps, xT_sb, hT_ps, hT_sb, pq_ps, pq_sb = map(sem, ("xT_ps", "xT_sb", "hT_ps", "hT_sb", "pq_ps", "pq_sb"))
        q_st = sem("q_st")
        tile_found, tile_rows = sem("tile_found"), sem("tile_rows")
        start_done, start_next = sem("start_done"), sem("start_next")
        full_done, full_sum = sem("full_done"), sem("full_sum")
        node_rows, p_scat = sem("node_rows"), sem("p_scat")
        idx_done = sem("idx_done")
        row_ld = [sem(f"row_ld{s}") for s in range(UN)]
        win_ld = [sem(f"win_ld{s}") for s in range(UN)]
        q_ld = [sem(f"q_ld{s}") for s in range(UN)]
        oh_done, m1_done, relu1, z_done, relu2, run_done, t_done, run_ev = map(
            sem, ("oh_done", "m1_done", "relu1", "z_done", "relu2", "run_done", "t_done", "run_ev"))
        run_st = [sem(f"run_st{s}") for s in range(UN)]
        dup_done, move_done = sem("dup_done"), sem("move_done")
        seg_ld = [sem(f"seg_ld{k}") for k in range(CH)]
        x1_sum, var_done, std_done, x1_done = map(sem, ("x1_sum", "var_done", "std_done", "x1_done"))
        res_done, res_st = sem("res_done"), sem("res_st")
        x1T_done, x1T_sb, y_done, y_sb, y_scat = map(sem, ("x1T_done", "x1T_sb", "y_done", "y_sb", "y_scat"))
        row2_ld = [sem(f"row2_ld{s}") for s in range(UN)]
        win2_ld = [sem(f"win2_ld{s}") for s in range(UN)]
        sel_done, mt_done, mt_ev, msg_done, msg_ev = map(sem, ("sel_done", "mt_done", "mt_ev", "msg_done", "msg_ev"))
        acc_add = [sem(f"acc_add{k}") for k in range(NACC)]
        acc_ld = [sem(f"acc_ld{k}") for k in range(len(acc_sb))]
        half_sum, other_half, acc_sum, var2_done, std2_done, out_done = map(
            sem, ("half_sum", "other_half", "acc_sum", "var2_done", "std2_done", "out_done"))
        out_st = [sem(f"out_st{k}") for k in range(len(acc_sb))]

        def grp(i, r):
            return UN * i + r

        def uses(i, r):
            return 2 * i + r // 2 + 1

        def i_of(i, r):
            return i + r // UN

        def runs(i, r):
            return not isinstance(i, int) or 0 <= UN * i + r < G

        def old(i, r):
            return not isinstance(i, int) or UN * i + r >= 0

        def outs(c):
            return sum(2 + (d * CH < LASTN) for d in range(c % len(acc_sb), c + 1, len(acc_sb)))

        node = lambda a: a.rearrange("(p h) d -> p h d", p=P)

        block = ctx.enter_context(nc.Block())

        @block.gpsimd
        def _(pool):
            nc.gpsimd.memset(zeros[:], 0.0).then_inc(zeros_set, 1)
            nc.gpsimd.memset(eps[:], EPS).then_inc(consts_a, 1)
            nc.gpsimd.memset(ident[:], 0.0).then_inc(consts_a, 1)
            nc.gpsimd.memset(before[:], 1.0).then_inc(consts_a, 1)
            nc.gpsimd.memset(after[:], 1.0).then_inc(consts_a, 1)
            nc.gpsimd.memset(shift[:], 0.0).then_inc(consts_a, 1)
            kw = dict(allow_small_or_imprecise_dtypes=True)
            nc.gpsimd.iota(iota_p[:], pattern=[[0, 1]], base=0, channel_multiplier=1, **kw).then_inc(consts, 1)
            nc.gpsimd.iota(iota_f[:], pattern=[[1, P]], base=0, channel_multiplier=0, **kw).then_inc(consts, 1)
            nc.gpsimd.iota(node_id[:], pattern=[[1, H]], base=0, channel_multiplier=H, **kw).then_inc(consts, 1)
            nc.gpsimd.iota(spare[:], pattern=[[1, H]], base=CROWS, channel_multiplier=H, **kw).then_inc(consts, 1)
            nc.gpsimd.iota(trash[:], pattern=[[0, 1]], base=NP, channel_multiplier=1, **kw).then_inc(consts, 1)
            pool.wait_ge(consts_a, 5)
            nc.gpsimd.affine_select(out=ident[:], in_=ident[:], compare_op=ALU.not_equal, fill=1.0, base=0,
                                    pattern=[[-1, P]], channel_multiplier=1).then_inc(consts, 1)
            nc.gpsimd.affine_select(out=before[:], in_=before[:], compare_op=ALU.is_gt, fill=0.0, base=0,
                                    pattern=[[-1, P]], channel_multiplier=1).then_inc(consts, 1)
            nc.gpsimd.affine_select(out=after[:], in_=after[:], compare_op=ALU.is_gt, fill=0.0, base=0,
                                    pattern=[[1, P]], channel_multiplier=-1).then_inc(consts, 1)
            nc.gpsimd.affine_select(out=shift[:], in_=shift[:], compare_op=ALU.not_equal, fill=1.0, base=-1,
                                    pattern=[[-1, P]], channel_multiplier=1).then_inc(consts, 1)

            pool.wait_ge(x_ld, 48)
            pool.wait_ge(pads_set, 6)
            nc.gpsimd.tensor_copy(qg[:, 0, :, :], x_sb[:, 0:GT, :]).then_inc(x_cols, 1)
            with pool.Fori(1, HX // GT) as g:
                pool.wait_ge(xT_ps, g)
                nc.gpsimd.tensor_copy(qg[:, 0, :, :], x_sb[:, ds(g * GT, GT), :]).then_inc(x_cols, 1)

            pool.wait_ge(tile_found, 1)
            pool.wait_ge(dst_st, 16)
            pool.wait_ge(q_st, 16)
            for h in range(H):
                pool.indirect_dma_start(rows[:, h, :], None, dst_tab[:, :], IOA(ap=tile_i[:, h:h + 1], axis=0)).then_inc(tile_rows, 16)
            pool.wait_ge(node_rows, 1)
            pool.wait_ge(pq_sb, 2 * (HX // GT))
            pool.wait_ge(c_zero, 16 * ZP)
            for h in range(H):
                pool.indirect_dma_start(c_tab[:, :], IOA(ap=crow_i[:, h:h + 1], axis=0), p_sb[:, h, :], None).then_inc(p_scat, 16)

            def gather(i, r):
                pool.wait_ge(idx_done, grp(i, r) + 1)
                if old(i, r - UN):
                    pool.wait_ge(m1_done, grp(i, r - UN) + 1)
                pool.sem_inc(pool_waited, 1)
                for j in range(GT):
                    pool.indirect_dma_start(qg[:, r, j, :], None, q_tab[:, :],
                                            IOA(ap=src_idx[:, r, j:j + 1], axis=0)).then_inc(q_ld[r], 16)

            for r in range(UN):
                gather(0, r)
            with pool.Fori(1, IT) as i:
                for r in range(UN):
                    gather(i, r)

            for s in range(UN):
                pool.wait_ge(run_st[s], 16 * IT)
            for h in range(H):
                pool.indirect_dma_start(rows[:, h, :], None, seg_tab[:, :],
                                        IOA(ap=end_i[:, h:h + 1], axis=0)).then_inc(seg_ld[h // CH], 16)
            for h in range(H):
                if h % CH == 0:
                    pool.wait_ge(y_sb, h // CH + 1)
                pool.indirect_dma_start(c_tab[:, :], IOA(ap=crow_i[:, h:h + 1], axis=0), y[:, h, :], None).then_inc(y_scat, 16)

            pool.wait_ge(acc_zero, 16 * ZP * NACC)
            pool.wait_ge(res_st, 16 * CH)

            def scatter(i, r):
                pool.wait_ge(idx_done, G + 2 + grp(i, r) + 1)
                pool.wait_ge(msg_ev, grp(i, r) + 1)
                for j in range(GT):
                    if old(i, r - 1):
                        pool.wait_ge(acc_add[j], 16 * grp(i, r))
                    pool.sem_inc(pool_waited, 1)
                    pool.indirect_dma_start(acc_tab[j][:, :], IOA(ap=src_idx[:, r, j:j + 1], axis=0), msg[:, r, j, :], None,
                                            compute_op=ALU.add).then_inc(acc_add[j], 16)

            for r in range(UN):
                scatter(0, r)
            with pool.Fori(1, IT) as i:
                for r in range(UN):
                    scatter(i, r)

            for c in range(CH):
                k = c % len(acc_sb)
                pool.wait_ge(acc_ld[k], 16 * NACC * (c // len(acc_sb) + 1))
                nc.gpsimd.tensor_tensor(acc_sb[k][:, 0:CH, :], acc_sb[k][:, 0:CH, :], acc_sb[k][:, CH:2 * CH, :], ALU.add).then_inc(half_sum, 1)

        @block.sync
        def _(sp):
            ev = lambda a: a[0:(PA - 1) * EPA].rearrange("(p j) -> p j", j=EPA)
            tail = lambda a: a[(PA - 1) * EPA:E].rearrange("(a j) -> a j", a=1)
            cut = 96
            sp.wait_ge(pads_set, 4)
            for a, sbuf, s in ((dst, dst_i, dst_ld), (src, src_i, src_ld), (edge_weight, w_a, w_ld)):
                sp.dma_start(sbuf[0:cut, :], ev(a)[0:cut, :]).then_inc(s, 16)
                sp.dma_start(sbuf[cut:PA - 1, :], ev(a)[cut:PA - 1, :]).then_inc(s, 16)
                sp.dma_start(sbuf[PA - 1:PA, 0:LASTE], tail(a)).then_inc(s, 16)
                if a is dst:
                    sp.dma_start(prev_i[1:PA, :], ev(a)[:, EPA - 1:EPA], allow_slow_non_contiguous=True).then_inc(s, 16)
            sp.wait_ge(pads_set, 6)
            xv = x[0:(P - 1) * H, :].rearrange("(p h) d -> p h d", h=H)
            sp.dma_start(x_sb[0:112, 0:H, :], xv[0:112, :, :]).then_inc(x_ld, 16)
            sp.dma_start(x_sb[112:P - 1, 0:H, :], xv[112:P - 1, :, :]).then_inc(x_ld, 16)
            sp.dma_start(x_sb[P - 1:P, 0:LASTN, :], x[(P - 1) * H:N, :].rearrange("(a h) d -> a h d", a=1)).then_inc(x_ld, 16)

            sp.wait_ge(tabs_ready, 1)
            sp.dma_start(dst_tab.rearrange("(p k) e -> p (k e)", p=PA), dst_f[:, :]).then_inc(dst_st, 16)
            sp.dma_start(last_tab.rearrange("a (p k) -> p (a k)", p=PA),
                         dst_f[:, :].rearrange("p (k e) -> p k e", e=P)[:, :, P - 1], allow_slow_non_contiguous=True).then_inc(back_ld, 16)
            sp.wait_ge(back_ld, 16)
            sp.dma_start(last_bc[:, :], last_tab.to_broadcast([P, T])).then_inc(back_ld, 16)
            sp.wait_ge(tabs_ready, 2)
            sp.dma_start(base_tab.rearrange("a (p k) -> p (a k)", p=PA), base_i[:, :], allow_slow_non_contiguous=True).then_inc(base_ld, 16)
            for a, sbuf in ((seg_row_tab[:, 0, :], rel_u8), (seg_row_tab[:, 1, :], cont_u8), (src_row_tab, src_u16)):
                sp.dma_start(a.rearrange("(p q) e -> p q e", p=PA), sbuf[:, :].rearrange("p (q e) -> p q e", e=GE)).then_inc(tabs_st, 16)
            sp.wait_ge(base_ld, 16)
            sp.dma_start(base_row[:, :], base_tab[:, :]).then_inc(base_ld, 16)
            sp.wait_ge(pq_sb, 2 * (HX // GT))
            sp.dma_start(node(q_tab), q_sb[:, 0:H, :]).then_inc(q_st, 16)
            sp.wait_ge(tabs_st, 48)
            sp.wait_ge(base_ld, 32)
            sp.wait_ge(p_scat, 16 * H)

            def windows(i, r, sems):
                sp.sem_inc(sp_waited, 1)
                _, bases = nc.values_load_multi_w_load_instructions(
                    base_row[0:1, ds(GT * grp(i, r), GT)], engines=bass.OrderedEngineSet([mybir.EngineType.SP]), min_val=0, max_val=NP,
                    skip_runtime_bounds_check_because="a count of segments opened before a tile is below the count of nodes")
                for j, base in enumerate(bases):
                    sp.dma_start(win[:, r, j, :], c_tab[ds(base, P), :]).then_inc(sems[r], 16)

            def load0(i, r):
                if old(i, r - UN):
                    sp.wait_ge(run_done, grp(i, r - UN) + 1)
                    sp.sem_inc(sp_waited, 1)
                sp.dma_start(row_bc[:, r, :], seg_row_tab.rearrange("g a e -> g (a e)")[ds(grp(i, r), 1), :].to_broadcast([P, 2 * GE])).then_inc(row_ld[r], 16)
                if old(i, r - UN):
                    sp.wait_ge(m1_done, grp(i, r - UN) + 1)
                windows(i, r, win_ld)

            for r in range(UN):
                load0(0, r)
            with sp.Fori(1, IT) as i:
                for r in range(UN):
                    load0(i, r)

            sp.wait_ge(acc_zero, 16 * ZP * NACC)
            for c in range(CH):
                sp.wait_ge(res_done, c + 1)
                sp.dma_start(node(acc_tab[0][0:NP, :])[:, c * CH:(c + 1) * CH, :], res[:, c * CH:(c + 1) * CH, :]).then_inc(res_st, 16)

            sp.wait_ge(y_scat, 16 * H)

            def load1(i, r):
                if old(i, r - UN):
                    sp.wait_ge(dup_done, grp(i, r - UN) + 1)
                    sp.sem_inc(sp_waited, 1)
                sp.dma_start(row_bc[:, r, :].bitcast(U16), src_row_tab[ds(grp(i, r), 1), :].to_broadcast([P, GE])).then_inc(row2_ld[r], 16)
                if old(i, r - UN):
                    sp.wait_ge(msg_done, grp(i, r - UN) + 1)
                windows(i, r, win2_ld)

            for r in range(UN):
                load1(0, r)
            with sp.Fori(1, IT) as i:
                for r in range(UN):
                    load1(i, r)

            for k in range(NACC):
                sp.wait_ge(acc_add[k], 16 * G)
            for c in range(CH):
                s = c % len(acc_sb)
                if c >= len(acc_sb):
                    sp.wait_ge(out_st[s], 16 * outs(c - len(acc_sb)))
                for k in range(NACC):
                    sp.dma_start(acc_sb[s][:, k * CH:(k + 1) * CH, :], node(acc_tab[k][0:NP, :])[:, c * CH:(c + 1) * CH, :]).then_inc(acc_ld[s], 16)
            for k in range(len(acc_sb)):
                last = max(c for c in range(CH) if c % len(acc_sb) == k)
                sp.wait_ge(out_st[k], 16 * outs(last))

        @block.scalar
        def _(act):
            for sbuf, a in ((w1[:], W1), (w2[:], W2.rearrange("(k p) d -> p k d", p=P)), (w3[:], W3), (wl[:], WL),
                            (bias[:, 0:1], b1.rearrange("(p a) -> p a", a=1)), (bias[:, 1:2], b2.rearrange("(p a) -> p a", a=1)),
                            (bias[:, 2:3], b3.rearrange("(p a) -> p a", a=1)),
                            (bl_bc[:], bL.rearrange("(a d) -> a d", a=1).to_broadcast([P, D]))):
                act.dma_start(sbuf, a).then_inc(wt_ld, 16)
            act.wait_ge(zeros_set, 1)
            for tab, s in [(c_tab, c_zero)] + [(a, acc_zero) for a in acc_tab]:
                v = tab[0:CROWS, :].rearrange("(p a r) d -> a p (r d)", p=P, a=ZP)
                for a in range(ZP):
                    act.dma_start(v[a], zeros[:, :]).then_inc(s, 16)
            act.wait_ge(tr_out, 1)
            nc.scalar.activation(wlT[:], s_ps[:, 1, 0:D], ACT.Copy).then_inc(tr_copied, 1)

            act.wait_ge(wt_ld, 16 * 8)
            with act.Fori(0, HX // GT) as g:
                act.wait_ge(xT_ps, g + 1)
                nc.scalar.activation(xT[:], m1_ps[:, 0, :], ACT.Copy).then_inc(xT_sb, 1)
                act.wait_ge(hT_ps, g + 1)
                nc.scalar.activation(hT[:], z_ps[:, 0, :], ACT.Identity, bias=bias[:, 0:1]).then_inc(hT_sb, 1)
                act.wait_ge(pq_ps, g + 1)
                pq = t_ps[:, :, :].rearrange("p a (b f) -> p (a b) f", f=2 * D)
                nc.scalar.activation(p_sb[:, ds(g * GT, GT), :], pq[:, :, 0:D], ACT.Copy).then_inc(pq_sb, 1)
                nc.scalar.activation(q_sb[:, ds(g * GT, GT), :], pq[:, :, D:2 * D], ACT.Copy).then_inc(pq_sb, 1)

            def relu_1(i, r):
                s = r % 2
                act.wait_ge(m1_done, grp(i, r) + 1)
                if old(i, r - 2):
                    act.wait_ge(z_done, grp(i, r - 2) + 1)
                nc.scalar.activation(m1[:, s, :], m1_ps[:, s, :], ACT.Relu, bias=bias[:, 1:2]).then_inc(relu1, 1)

            def relu_2(i, r):
                s = r % 2
                act.wait_ge(z_done, grp(i, r) + 1)
                if old(i, r - 2):
                    act.wait_ge(run_done, grp(i, r - 2) + 1)
                nc.scalar.activation(m2[:, s, :], z_ps[:, s, :], ACT.Relu, bias=bias[:, 2:3]).then_inc(relu2, 1)

            def store(i, r):
                act.wait_ge(t_done, grp(i, r) + 1)
                if old(i, r - UN):
                    act.wait_ge(run_st[r % UN], 16 * i_of(i, r))
                nc.scalar.activation(run_e[:, r % UN, :, :], t_ps[:, r % 2, :].rearrange("p (t d) -> p t d", d=D), ACT.Copy).then_inc(run_ev, 1)
                act.wait_ge(run_ev, grp(i, r) + 1)
                act.dma_start(seg_tab.rearrange("(g t e) d -> g e t d", e=P, t=GT)[ds(grp(i, r), 1)].rearrange("a e t d -> (a e) t d"),
                              run_e[:, r % UN, :, :]).then_inc(run_st[r % UN], 16)

            def step0(i, r):
                for part, lag in ((relu_1, 0), (relu_2, 1), (store, 3)):
                    if runs(i, r - lag):
                        part(i, r - lag)

            for r in range(UN):
                step0(0, r)
            with act.Fori(1, IT) as i:
                for r in range(UN):
                    step0(i, r)
            for r in range(3):
                step0(IT, r)

            def root(c, var, done):
                act.wait_ge(var, c + 1)
                cols = slice(c * CH, (c + 1) * CH)
                nc.scalar.activation(std[:, cols], mv[:, cols, 1], ACT.Sqrt, bias=eps[:]).then_inc(done, 1)

            for c in range(CH + 2):
                if c < CH:
                    root(c, var_done, std_done)
                if 1 <= c <= CH:
                    act.wait_ge(x1T_done, c)
                    if c >= 3:
                        act.wait_ge(y_done, c - 2)
                    nc.scalar.activation(x1T[(c - 1) % 2][:, 0:CH, :], x1T_ps[(c - 1) % 2][:, 0:CH, :], ACT.Copy).then_inc(x1T_sb, 1)
                if c >= 2:
                    act.wait_ge(y_done, c - 1)
                    nc.scalar.activation(y[:, (c - 2) * CH:(c - 1) * CH, :], y_ps[c % 2][:, 0:CH, :], ACT.Copy).then_inc(y_sb, 1)

            def mix_ev(i, r):
                s = r % 2
                act.wait_ge(mt_done, grp(i, r) + 1)
                if old(i, r - 2):
                    act.wait_ge(msg_done, grp(i, r - 2) + 1)
                nc.scalar.activation(m1[:, s, :], m1_ps[:, s, :], ACT.Copy).then_inc(mt_ev, 1)

            def message_ev(i, r):
                s = r % 2
                act.wait_ge(msg_done, grp(i, r) + 1)
                if old(i, r - UN):
                    for k in range(NACC):
                        act.wait_ge(acc_add[k], 16 * (grp(i, r - UN) + 1))
                nc.scalar.activation(msg[:, r % UN, :, :], z_ps[:, s, :].rearrange("p (t d) -> p t d", d=D), ACT.Copy).then_inc(msg_ev, 1)

            def step1(i, r):
                if runs(i, r):
                    mix_ev(i, r)
                if runs(i, r - 1):
                    message_ev(i, r - 1)

            for r in range(UN):
                step1(0, r)
            with act.Fori(1, IT) as i:
                for r in range(UN):
                    step1(i, r)
            step1(IT, 0)

            xv = out[0:(P - 1) * H, :].rearrange("(p h) d -> p h d", h=H)
            for c in range(CH + 1):
                if c < CH:
                    root(c, var2_done, std2_done)
                if c >= 1:
                    act.wait_ge(out_done, c)
                    a, b = (c - 1) * CH, c * CH
                    s = (c - 1) % len(acc_sb)
                    act.dma_start(xv[0:112, a:b, :], acc_sb[s][0:112, 0:CH, :]).then_inc(out_st[s], 16)
                    act.dma_start(xv[112:P - 1, a:b, :], acc_sb[s][112:P - 1, 0:CH, :]).then_inc(out_st[s], 16)
                    n = min(b, LASTN) - a
                    if n > 0:
                        act.dma_start(out[(P - 1) * H + a:(P - 1) * H + a + n, :].rearrange("(a h) d -> a h d", a=1),
                                      acc_sb[s][P - 1:P, 0:n, :]).then_inc(out_st[s], 16)

        @block.vector
        def _(dve):
            chain = [0]

            def link(ins):
                chain[0] += 1
                ins.then_inc(dve_own, 1)
                dve.wait_ge(dve_own, chain[0])

            V = nc.vector
            V.memset(prev_i[:], -1).then_inc(pads_set, 1)
            V.memset(dst_i[:], N).then_inc(pads_set, 1)
            V.memset(src_i[:], N).then_inc(pads_set, 1)
            V.memset(w_a[:], 0.0).then_inc(pads_set, 1)
            V.memset(x_sb[:, H:HX, :], 0.0).then_inc(pads_set, 1)
            V.memset(x_sb[96:P, LASTN:H, :], 0.0).then_inc(pads_set, 1)
            link(V.memset(src_ti[:, T:], 0))

            dve.wait_ge(dst_ld, 64)
            V.tensor_copy(dst_f[:], dst_i[:]).then_inc(tabs_ready, 1)
            dve.wait_ge(tabs_ready, 1)
            link(V.tensor_copy(prev_f[:], prev_i[:]))
            V.tensor_tensor(cont[:, 1:], dst_f[:, 1:], dst_f[:, :EPA - 1], ALU.is_equal)
            link(V.tensor_tensor(cont[:, 0:1], dst_f[:, 0:1], prev_f[:], ALU.is_equal))
            V.tensor_copy(cont_u8[:], cont[:])
            link(V.tensor_scalar(opens[:], cont[:], -1.0, 1.0, ALU.mult, ALU.add))
            V.tensor_tensor_scan(cid[:], opens[:], opens[:], 0.0, ALU.add, ALU.max).then_inc(opens_done, 1)
            dve.wait_ge(src_ld, 48)
            V.tensor_copy(src_f[:], src_i[:]).then_inc(tr_in, 1)
            V.tensor_copy(src_u16[:], src_i[:])
            dve.wait_ge(wt_ld, 16 * 8)
            V.tensor_tensor(wpq[:, 0, :], w2[:, 0, :], w2[:, 1, :], ALU.subtract)
            V.tensor_copy(wpq[:, 1, :], w2[:, 1, :]).then_inc(wpq_done, 1)
            dve.wait_ge(cid_sum, 1)
            link(V.tensor_scalar(cid_off[:], s_ps[0:PA, 0, 0:1], -1.0, None, ALU.add))
            link(V.tensor_scalar(cid[:], cid[:], cid_off[:], None, ALU.add))
            cidv = cid[:, :].rearrange("p (k e) -> p k e", e=P)
            V.tensor_copy(base_i[:], cidv[:, :, 0])
            link(V.tensor_copy(base_f[:], cidv[:, :, 0]))
            link(V.tensor_tensor(rel[:, :].rearrange("p (k e) -> p k e", e=P), cidv,
                                 base_f[:, :].unsqueeze(2).to_broadcast([PA, TA, P]), ALU.subtract))
            V.tensor_copy(rel_u8[:], rel[:]).then_inc(tabs_ready, 1)
            V.tensor_copy(tmp_h[:, 0:1], iota_p[:]).then_inc(tr_in, 1)

            tv = lambda a: a.rearrange("p (q k) -> p k q", k=TA)
            pv = s_ps[:, :, :].rearrange("p a (b q) -> p (a b) q", q=P)[:, 0:TA, 0:PA]
            dve.wait_ge(tr_out, 2)
            V.tensor_copy(tv(src_t[:, :]), pv)
            link(V.tensor_copy(tv(src_ti[:, 0:T]), pv))
            V.tensor_scalar(to_trash[:], src_t[:], -1.0, trash[:], ALU.mult, ALU.add)
            V.tensor_copy(tmp_h[:, 0:1], iota_p[:]).then_inc(tr_copied, 1)
            dve.wait_ge(tr_out, 3)
            V.tensor_copy(tv(w_t[:, :]), pv).then_inc(tr_copied, 1)
            dve.wait_ge(tr_out, 4)
            V.tensor_copy(tv(rel_t[:, :]), pv).then_inc(tr_copied, 1)

            dve.wait_ge(back_ld, 32)
            dve.wait_ge(consts, 9)
            with dve.Fori(0, H) as h:
                V.tensor_scalar(tmp_t[:], last_bc[:], node_id[:, ds(h, 1)], None, ALU.is_lt, ALU.add,
                                accum_out=tile_of[:, ds(h, 1)]).then_inc(counted, 1)
                dve.wait_ge(counted, h + 1)
            link(V.tensor_scalar(tile_of[:], tile_of[:], float(T - 1), None, ALU.min))
            V.tensor_copy(tile_i[:], tile_of[:]).then_inc(tile_found, 1)
            dve.wait_ge(tile_rows, 16 * H)
            link(V.tensor_tensor(rows[:, 0:H, :], rows[:, 0:H, :], node_id[:, :].unsqueeze(2).to_broadcast([P, H, P]), ALU.is_lt))
            link(V.tensor_reduce(start[:], rows[:, 0:H, :], axis=AX_X, op=ALU.add))
            V.scalar_tensor_tensor(start[:], tile_of[:], float(P), start[:], ALU.mult, ALU.add).then_inc(start_done, 1)
            dve.wait_ge(start_next, 1)
            V.tensor_copy(end[:, 0:H - 1], start[:, 1:H])
            link(V.tensor_copy(end[:, H - 1:H], s_ps[:, 1, 0:1]))
            link(V.tensor_tensor(full[:], end[:], start[:], ALU.is_gt))
            V.tensor_tensor_scan(seg[:], full[:], full[:], 0.0, ALU.add, ALU.max).then_inc(full_done, 1)
            link(V.tensor_scalar(tmp_h[:], end[:], -1.0, 0.0, ALU.add, ALU.max))
            V.tensor_copy(end_i[:], tmp_h[:])
            dve.wait_ge(full_sum, 1)
            link(V.tensor_scalar(seg_off[:], s_ps[:, 1, 1:2], -1.0, None, ALU.add))
            link(V.scalar_tensor_tensor(seg[:], seg[:], seg_off[:], spare[:], ALU.add, ALU.subtract))
            link(V.tensor_tensor(seg[:], seg[:], full[:], ALU.mult))
            link(V.tensor_tensor(seg[:], seg[:], spare[:], ALU.add))
            V.tensor_copy(crow_i[:], seg[:]).then_inc(node_rows, 1)

            def indices(i, r):
                V.tensor_copy(src_idx[:, r % UN, :], src_ti[:, ds(GT * grp(i, r), GT)]).then_inc(idx_done, 1)

            def one_hot(i, r):
                s = r % 2
                dve.wait_ge(row_ld[r % UN], 16 * (i + 1))
                if old(i, r - 2):
                    dve.wait_ge(m1_done, grp(i, r - 2) + 1)
                V.tensor_scalar(oh[:, s, :], row_bc[:, r % UN, 0:GE], iota_p[:], None, ALU.is_equal).then_inc(oh_done, 1)

            def scan(i, r):
                s = r % 2
                dve.wait_ge(relu2, grp(i, r) + 1)
                if old(i, r - 2):
                    dve.wait_ge(t_done, grp(i, r - 2) + 1)
                first = 0.0
                if old(i, r - 1):
                    dve.wait_ge(run_done, grp(i, r))
                    first = run[:, 1 - s, GE - 1:GE]
                V.tensor_tensor_scan(run[:, s, :], row_bc[:, r % UN, GE:2 * GE], m2[:, s, :], first, ALU.mult, ALU.max).then_inc(run_done, 1)

            def step0(i, r):
                if runs(i, r):
                    if old(i, r - 2):
                        dve.wait_ge(q_ld[(r - 2) % UN], 16 * GT * (i_of(i, r - 2) + 1))
                    indices(i, r + 2)
                    one_hot(i, r)
                if runs(i, r - 2):
                    scan(i + (r - 2) // UN if isinstance(i, int) else i, (r - 2) % UN if isinstance(i, int) else r - 2)

            indices(0, 0)
            indices(0, 1)
            for r in range(UN):
                step0(0, r)
            with dve.Fori(1, IT) as i:
                for r in range(UN):
                    step0(i, r)
            for r in range(2):
                step0(IT, r)

            def moments(c, v, done):
                for h in range(CH):
                    last = V.bn_stats(part[:, h, :], v[:, h, :])
                link(last)
                for h in range(CH):
                    last = V.bn_aggr(mv[:, c * CH + h, :], part[:, h, :])
                last.then_inc(done, 1)

            def normalise(c, v, rooted, done):
                cols = slice(c * CH, (c + 1) * CH)
                dve.wait_ge(rooted, c + 1)
                link(V.reciprocal(rstd[:, cols], std[:, cols]))
                for h in range(CH):
                    n = c * CH + h
                    last = V.tensor_scalar(v[:, h, :], v[:, h, :], mv[:, n, 0:1], rstd[:, n:n + 1], ALU.subtract, ALU.mult)
                last.then_inc(done, 1)

            for c in range(CH + 1):
                if c < CH:
                    dve.wait_ge(seg_ld[c], 16 * CH)
                    for h in range(c * CH, (c + 1) * CH):
                        last = V.scalar_tensor_tensor(x1[:, h, :], rows[:, h, :], full[:, h:h + 1], x_sb[:, h, :], ALU.mult, ALU.add)
                    last.then_inc(x1_sum, 1)
                    dve.wait_ge(x1_sum, c + 1)
                    moments(c, x1[:, c * CH:(c + 1) * CH, :], var_done)
                if c >= 1:
                    v = x1[:, (c - 1) * CH:c * CH, :]
                    normalise(c - 1, v, std_done, x1_done)
                    dve.wait_ge(x1_done, c)
                    V.tensor_tensor(res[:, (c - 1) * CH:c * CH, :], v, bl_bc[:, :].unsqueeze(1).to_broadcast([P, CH, D]), ALU.add).then_inc(res_done, 1)

            def selections(i, r):
                s = r % 2
                dve.wait_ge(row2_ld[r], 16 * (i + 1))
                if old(i, r - 2):
                    dve.wait_ge(mt_done, grp(i, r - 2) + 1)
                V.tensor_tensor(oh[:, s, :].rearrange("p (t c) -> p t c", c=P), iota_f[:, :].unsqueeze(1).to_broadcast([P, GT, P]),
                                rel_t[:, ds(GT * grp(i, r), GT)].unsqueeze(2).to_broadcast([P, GT, P]), ALU.is_equal)
                src16 = row_bc[:, r, :].bitcast(U16)
                tile_src = lambda j: (src16[:, j * P:(j + 1) * P], src_t[:, ds(GT * grp(i, r) + j, 1)])
                for j in range(GT):
                    row, col = tile_src(j)
                    last = V.tensor_scalar(sel[:, s, j * P:(j + 1) * P], row, col, w_t[:, ds(GT * grp(i, r) + j, 1)], ALU.is_equal, ALU.mult)
                last.then_inc(sel_done, 1)
                if old(i, r - 1):
                    dve.wait_ge(idx_done, G + 2 + grp(i, r))
                for j in range(GT):
                    row, col = tile_src(j)
                    last = V.scalar_tensor_tensor(junk[:, j, :], row, col, before[:], ALU.is_equal, ALU.mult, accum_out=dup[:, j:j + 1])
                last.then_inc(dup_done, 1)

            def accumulator_rows(i, r):
                dve.wait_ge(dup_done, grp(i, r) + 1)
                V.scalar_tensor_tensor(move[:], dup[:], 0.5, to_trash[:, ds(GT * grp(i, r), GT)], ALU.is_gt, ALU.mult).then_inc(move_done, 1)
                if old(i, r - UN):
                    for k in range(NACC):
                        dve.wait_ge(acc_add[k], 16 * (grp(i, r - UN) + 1))
                dve.wait_ge(move_done, grp(i, r) + 1)
                V.tensor_tensor(src_idx[:, r, :], move[:], src_t[:, ds(GT * grp(i, r), GT)], ALU.add).then_inc(idx_done, 1)

            def step1(i, r):
                selections(i, r)
                accumulator_rows(i, r)

            for r in range(UN):
                step1(0, r)
            with dve.Fori(1, IT) as i:
                for r in range(UN):
                    step1(i, r)

            for c in range(CH + 1):
                if c < CH:
                    k = c % len(acc_sb)
                    a = acc_sb[k]
                    dve.wait_ge(acc_ld[k], 16 * NACC * (c // len(acc_sb) + 1))
                    V.tensor_tensor(a[:, 2 * CH:3 * CH, :], a[:, 2 * CH:3 * CH, :], a[:, 3 * CH:4 * CH, :], ALU.add).then_inc(other_half, 1)
                    dve.wait_ge(half_sum, c + 1)
                    dve.wait_ge(other_half, c + 1)
                    V.tensor_tensor(a[:, 0:CH, :], a[:, 0:CH, :], a[:, 2 * CH:3 * CH, :], ALU.add).then_inc(acc_sum, 1)
                    dve.wait_ge(acc_sum, c + 1)
                    moments(c, a[:, 0:CH, :], var2_done)
                if c >= 1:
                    normalise(c - 1, acc_sb[(c - 1) % len(acc_sb)][:, 0:CH, :], std2_done, out_done)

        @block.tensor
        def _(pe):
            mm = nc.tensor.matmul
            pe.wait_ge(consts, 9)
            pe.wait_ge(wt_ld, 16 * 8)
            nc.tensor.transpose(s_ps[:, 1, 0:D], wl[:], ident[:]).then_inc(tr_out, 1)
            pe.wait_ge(opens_done, 1)
            mm(s_ps[0:PA, 0, 0:1], lhsT=after[0:PA, 0:PA], rhs=cid[:, EPA - 1:EPA], start=True, stop=True).then_inc(cid_sum, 1)

            def by_tile(a, n):
                for k in range(TA):
                    last = nc.tensor.transpose(s_ps[:, k // 4, (k % 4) * P:(k % 4) * P + PA], a[:, k * P:(k + 1) * P], ident[0:PA, 0:PA])
                last.then_inc(tr_out, 1)

            pe.wait_ge(tr_in, 2)
            pe.wait_ge(tr_copied, 1)
            by_tile(src_f, 1)
            pe.wait_ge(w_ld, 48)
            pe.wait_ge(tr_copied, 2)
            by_tile(w_a, 2)
            pe.wait_ge(tr_copied, 3)
            by_tile(rel, 3)

            pe.wait_ge(wpq_done, 1)
            pq = t_ps[:, :, :].rearrange("p a (b f) -> p (a b) f", f=2 * D)
            with pe.Fori(0, HX // GT) as g:
                pe.wait_ge(x_cols, g + 1)
                for j in range(GT):
                    last = nc.tensor.transpose(m1_ps[:, 0, j * P:(j + 1) * P], qg[:, 0, j, :], ident[:])
                last.then_inc(xT_ps, 1)
                pe.wait_ge(xT_sb, g + 1)
                mm(z_ps[:, 0, :], lhsT=w1[:], rhs=xT[:], start=True, stop=True).then_inc(hT_ps, 1)
                pe.wait_ge(hT_sb, g + 1)
                for j in range(GT):
                    last = mm(pq[:, j, :], lhsT=hT[:, j * P:(j + 1) * P], rhs=wpq[:, :, :].rearrange("p a d -> p (a d)"), start=True, stop=True)
                last.then_inc(pq_ps, 1)
                pe.wait_ge(pq_sb, 2 * g + 2)

            pe.wait_ge(start_done, 1)
            pe.wait_ge(tr_copied, 4)
            mm(s_ps[:, 1, 0:1], lhsT=shift[:], rhs=start[:, 0:1], start=True, stop=True).then_inc(start_next, 1)
            pe.wait_ge(full_done, 1)
            mm(s_ps[:, 1, 1:2], lhsT=after[:], rhs=seg[:, H - 1:H], start=True, stop=True).then_inc(full_sum, 1)

            def gathered(i, r):
                s = r % 2
                pe.wait_ge(q_ld[r], 16 * GT * (i + 1))
                pe.wait_ge(win_ld[r], 16 * GT * (i + 1))
                pe.wait_ge(oh_done, grp(i, r) + 1)
                if old(i, r - 2):
                    pe.wait_ge(relu1, grp(i, r - 2) + 1)
                for j in range(GT):
                    c = slice(j * P, (j + 1) * P)
                    mm(m1_ps[:, s, c], lhsT=qg[:, r, j, :], rhs=ident[:], start=True, stop=False)
                    last = mm(m1_ps[:, s, c], lhsT=win[:, r, j, :], rhs=oh[:, s, c], start=False, stop=True)
                last.then_inc(m1_done, 1)

            def second(i, r):
                s = r % 2
                pe.wait_ge(relu1, grp(i, r) + 1)
                if old(i, r - 2):
                    pe.wait_ge(relu2, grp(i, r - 2) + 1)
                mm(z_ps[:, s, :], lhsT=w3[:], rhs=m1[:, s, :], start=True, stop=True).then_inc(z_done, 1)

            def by_edge(i, r):
                s = r % 2
                pe.wait_ge(run_done, grp(i, r) + 1)
                if old(i, r - 2):
                    pe.wait_ge(run_ev, grp(i, r - 2) + 1)
                for j in range(GT):
                    c = slice(j * P, (j + 1) * P)
                    last = nc.tensor.transpose(t_ps[:, s, c], run[:, s, c], ident[:])
                last.then_inc(t_done, 1)

            def step0(i, r):
                for part, lag in ((gathered, 0), (second, 1), (by_edge, 3)):
                    if runs(i, r - lag):
                        part(i, r - lag)

            for r in range(UN):
                step0(0, r)
            with pe.Fori(1, IT) as i:
                for r in range(UN):
                    step0(i, r)
            for r in range(3):
                step0(IT, r)

            for c in range(CH + 1):
                if c < CH:
                    pe.wait_ge(x1_done, c + 1)
                    if c >= 2:
                        pe.wait_ge(x1T_sb, c - 1)
                    for h in range(CH):
                        last = nc.tensor.transpose(x1T_ps[c % 2][:, h, :], x1[:, c * CH + h, :], ident[:])
                    last.then_inc(x1T_done, 1)
                if c >= 1:
                    pe.wait_ge(x1T_sb, c)
                    if c >= 3:
                        pe.wait_ge(y_sb, c - 2)
                    for h in range(CH):
                        last = mm(y_ps[(c - 1) % 2][:, h, :], lhsT=x1T[(c - 1) % 2][:, h, :], rhs=wlT[:], start=True, stop=True)
                    last.then_inc(y_done, 1)

            def mix(i, r):
                s = r % 2
                pe.wait_ge(sel_done, grp(i, r) + 1)
                if old(i, r - 2):
                    pe.wait_ge(mt_ev, grp(i, r - 2) + 1)
                for j in range(GT):
                    c = slice(j * P, (j + 1) * P)
                    last = mm(m1_ps[:, s, c], lhsT=oh[:, s, c], rhs=sel[:, s, c], start=True, stop=True)
                last.then_inc(mt_done, 1)

            def message(i, r):
                s = r % 2
                pe.wait_ge(mt_ev, grp(i, r) + 1)
                pe.wait_ge(win2_ld[r % UN], 16 * GT * (i_of(i, r) + 1))
                if old(i, r - 2):
                    pe.wait_ge(msg_ev, grp(i, r - 2) + 1)
                for j in range(GT):
                    c = slice(j * P, (j + 1) * P)
                    last = mm(z_ps[:, s, c], lhsT=m1[:, s, c], rhs=win[:, r % UN, j, :], start=True, stop=True)
                last.then_inc(msg_done, 1)

            def step1(i, r):
                if runs(i, r):
                    mix(i, r)
                if runs(i, r - 1):
                    message(i, r - 1)

            for r in range(UN):
                step1(0, r)
            with pe.Fori(1, IT) as i:
                for r in range(UN):
                    step1(i, r)
            step1(IT, 0)


_INS = ["x", "src", "dst", "edge_weight", "L0_gnn_W1", "L0_gnn_b1", "L0_gnn_W2", "L0_gnn_b2", "L0_gnn_W3", "L0_gnn_b3",
        "L1_gnn_W", "L1_gnn_b"]


def kernel(**inputs):
    import numpy as np
    import concourse.bacc as bacc
    from concourse.bass_utils import run_bass_kernel_spmd

    nc = bacc.Bacc("TRN2", target_bir_lowering=False, num_devices=1)
    arrays, args = {}, []
    for name in _INS:
        a = np.ascontiguousarray(inputs[name])
        arrays[f"in_{name}_dram"] = a
        args.append(nc.dram_tensor(f"in_{name}_dram", a.shape, mybir.dt.from_np(a.dtype), kind="ExternalInput").ap())
    out = nc.dram_tensor("out_dram", (N, D), F32, kind="ExternalOutput").ap()
    gnn_kernel(nc, *args, out)
    r = run_bass_kernel_spmd(nc, [arrays], core_ids=[0])
    return r.results[0]["out_dram"]
```

```python
import concourse.bass as bass
from concourse import mybir
from contextlib import ExitStack

P = 128
D = 128
N = 6250
E = 100000
H = -(-N // P)
NP = P * H
HX = -(-H // 4) * 4
GT = 4
GE = GT * P
TA = 2 * GT
PA = 98
T = PA * TA
EP = T * P
G = T // GT
UN = 4
IT = G // UN
RING = 3 * UN
ITR = G // RING
EPA = TA * P
LASTN = N - (H - 1) * P
LASTE = E - (PA - 1) * EPA
CH = 7
CN = CH * P
NORM = [8, 8, 8, 8, 8, 6, 3]
NC = len(NORM)
XL = 16
CROWS = NP + P
NACC = GT
NB = -(-H // GT)
ZR = 4 * P
SPLIT = 4
EPS = 1e-5
AHEAD = RING - 1
WEIGHTS, CONSTS = 6, 12
assert sum(NORM) == H and SPLIT * CH % GT == 0 and H == CH * CH and G % UN == 0 and ZR % P == 0 and 0 < LASTE <= EPA and 0 < LASTN <= P

ALU = mybir.AluOpType
ACT = mybir.ActivationFunctionType
AX_X = mybir.AxisListType.X
F32 = mybir.dt.float32
I32 = mybir.dt.int32
U8 = mybir.dt.uint8
U16 = mybir.dt.uint16


def gnn_kernel(nc, x, src, dst, edge_weight, W1, b1, W2, b2, W3, b3, WL, bL, out):
    ds = bass.ds
    IOA = bass.IndirectOffsetOnAxis
    with ExitStack() as ctx:
        def sb(name, shape, dt=F32):
            return ctx.enter_context(nc.sbuf_tensor(name, shape, dt))

        def psum(name, shape):
            return ctx.enter_context(nc.psum_tensor(name, shape, F32))

        def sem(name):
            return ctx.enter_context(nc.semaphore(name))

        def dram(name, shape, dt=F32):
            return nc.dram_tensor(name, shape, dt, kind="Internal").ap()

        q_tab = dram("q_tab", [NP, D])
        seg_tab = dram("seg_tab", [EP, D])
        acc_tab = [dram(f"acc_tab{k}", [CROWS, D]) for k in range(NACC)]
        dst_tab = dram("dst_tab", [T, P])
        base_tab = dram("base_tab", [1, T], I32)
        seg_row_tab = dram("seg_row_tab", [G, 2, GE], U8)
        src_row_tab = dram("src_row_tab", [G, GE], U16)

        ident = sb("ident", [P, P])
        before = sb("before", [P, P])
        after = sb("after", [P, P])
        shift = sb("shift", [P, P])
        corner = sb("corner", [P, P])
        ones = sb("ones", [P, P])
        iota_n = sb("iota_n", [P, CN])
        chunk_at = sb("chunk_at", [P, CH])
        iota_p = sb("iota_p", [P, 1])
        iota_f = sb("iota_f", [P, P])
        node_id = sb("node_id", [P, H])
        trash = sb("trash", [P, 1])
        zeros = sb("zeros", [P, ZR // P * D])

        w1 = sb("w1", [P, D])
        w2 = sb("w2", [P, 2, D])
        wpq = sb("wpq", [P, 2, D])
        w3 = sb("w3", [P, D])
        wl = sb("wl", [P, D])
        wT = sb("wT", [P, 2, D])
        wlT = wT[:, 1, :]
        wf = sb("wf", [P, 2, D])
        bias = sb("bias", [P, 3])
        bias12 = sb("bias12", [P, 1])
        bl_bc = sb("bl_bc", [P, D])

        whole = sb("whole", [P, 3 * HX * D + 8 * EPA])
        x_sb, p_sb, q_sb = (whole[:, k * HX * D:(k + 1) * HX * D].rearrange("p (h d) -> p h d", d=D) for k in range(3))
        edge_part = [whole[0:PA, 3 * HX * D + k * EPA:3 * HX * D + (k + 1) * EPA] for k in range(8)]
        dst_i, src_i = (a.bitcast(I32) for a in edge_part[0:2])
        dst_f, cid, src_f, cont, w_a, rel = edge_part[2:]
        qg = whole[:, 3 * HX * D:3 * HX * D + RING * GE].rearrange("p (r t d) -> p r t d", t=GT, d=D)
        norm_cols = [slice(sum(NORM[:c]), sum(NORM[:c + 1])) for c in range(NC)]
        chunk_of = [c for c in range(NC) for _ in range(NORM[c])]
        acc_sb = [whole[:, NACC * D * n.start:NACC * D * n.stop].rearrange("p (k h d) -> p k h d", k=NACC, d=D) for n in norm_cols]

        prev_i = sb("prev_i", [PA, 1], I32)
        prev_f = sb("prev_f", [PA, 1])
        cid_off = sb("cid_off", [PA, 1])
        base_f = sb("base_f", [PA, TA])
        base_i = sb("base_i", [PA, TA], I32)
        opens = rel
        rel_u8 = sb("rel_u8", [PA, EPA], U8)
        cont_u8 = sb("cont_u8", [PA, EPA], U8)
        src_u16 = sb("src_u16", [PA, EPA], U16)
        base_row = sb("base_row", [1, T], I32)
        lasts = sb("lasts", [PA, TA + 1])
        prev_c = sb("prev_c", [PA, CH])
        last_c = sb("last_c", [PA, CH])
        src_t = sb("src_t", [P, T])
        src_ti = sb("src_ti", [P, T + AHEAD * GT], I32)
        rel_t = sb("rel_t", [P, T])
        w_t = sb("w_t", [P, T])
        to_trash = sb("to_trash", [P, T])

        rows = q_sb
        x1 = p_sb
        compact_T = [a.rearrange("p h d -> p (h d)") for a in (q_sb, x_sb)]
        res = q_sb
        tile_of = sb("tile_of", [P, H])
        tile_i = sb("tile_i", [P, H], I32)
        tile_less = sb("tile_less", [P, 2, CH, TA])
        tile_in = sb("tile_in", [P, H])
        below = sb("below", [P, H])
        start = sb("start", [P, H + 1])
        full = sb("full", [P, H])
        in_col = sb("in_col", [P, H])
        col_full = sb("col_full", [P, H])
        col_off = sb("col_off", [P, H])
        col_off_i = sb("col_off_i", [P, HX], I32)
        end_i = sb("end_i", [P, H], I32)
        part = sb("part", [P, max(NORM), 6])
        mv = sb("mv", [P, H, 2])
        std = sb("std", [P, H])
        rstd = sb("rstd", [P, H])
        shift_by = sb("shift_by", [P, H])
        eps = sb("eps", [P, 1])

        src_idx = sb("src_idx", [P, RING, GT], I32)
        row_bc = sb("row_bc", [P, UN, 2 * GE], U8)
        win_cols = sb("win_cols", [P, 2, GE])
        win = sb("win", [P, UN, GT, D])
        oh = sb("oh", [P, 2, GE])
        junk = sb("junk", [P, GT, P])
        dup = sb("dup", [P, GT])
        move = sb("move", [P, GT])
        m1 = sb("m1", [P, 2, GE])
        m2 = sb("m2", [P, 2, GE])
        run = sb("run", [P, 2, GE])
        run_e = sb("run_e", [P, UN, GT, D])
        sel = m2
        msg = run_e
        spare_rows = sb("spare_rows", [P, CH, D])
        halves = lambda a: a[:, :, :, :].rearrange("p (s a) b d -> p s (a b d)", s=2)
        above = halves(run_e)
        node_oh = halves(win)
        xT = oh
        cols_of = lambda a: [a[:, k * D:(k + 1) * D] for k in range(a.shape[1] // D)]
        hot = [c for a in (win[:, :, :, :].rearrange("p a t d -> p (a t d)"), oh[:, :, :].rearrange("p a e -> p (a e)"),
                           run[:, :, :].rearrange("p a e -> p (a e)"), junk[:, :, :].rearrange("p t d -> p (t d)"),
                           run_e[:, :, :, :].rearrange("p a t d -> p (a t d)")) for c in cols_of(a)]
        hot_late = len(hot) - UN * GT

        m1_ps = psum("m1_ps", [P, 2, GE])
        z_ps = psum("z_ps", [P, 2, GE])
        t_ps = psum("t_ps", [P, 2, GE])
        s_ps = psum("s_ps", [P, 2, GE])
        by_col = lambda a: a[:, :, :].rearrange("p a (b d) -> p (a b) d", d=D)
        by_block = lambda a: a.rearrange("p (b d) -> p b d", d=D)
        place_ps = [m1_ps[:, 0, :], m1_ps[:, 1, :], z_ps[:, 0, :], z_ps[:, 1, :]]
        pq_banks = [t_ps, z_ps]
        tile_ps = [s_ps, t_ps, s_ps]
        edge_rows = [by_col(m1), by_col(m2), by_col(run), spare_rows,
                     row_bc[:, :, :].rearrange("p a e -> p (a e)").bitcast(F32).rearrange("p (h d) -> p h d", d=D)]
        lasts_v = lambda c: s_ps[:, c % 2, 0:CH * (TA + 1)].rearrange("p (h k) -> p h k", k=TA + 1)
        end_ps, in_col_ps, col_full_ps = s_ps[:, 1, 0:H], s_ps[:, 0, 0:H], s_ps[:, 0, H:2 * H]

        pads_set = sem("pads_set")
        dst_ld, src_ld, w_ld, wt_ld = map(sem, ("dst_ld", "src_ld", "w_ld", "wt_ld"))
        x_ld = [sem(f"x_ld{k}") for k in range(-(-H // XL))]
        zeros_set, acc_zero = sem("zeros_set"), sem("acc_zero")
        consts_a, consts = sem("consts_a"), sem("consts")
        dve_own, counted = sem("dve_own"), sem("counted")
        pool_waited, sp_waited = sem("pool_waited"), sem("sp_waited")
        opens_done, cid_sum = sem("opens_done"), sem("cid_sum")
        tabs_ready, dst_st, tabs_st = sem("tabs_ready"), sem("dst_st"), sem("tabs_st")
        base_ld = sem("base_ld")
        src_ready, tr_out, tr_copied = sem("src_ready"), sem("tr_out"), sem("tr_copied")
        wpq_done, wT_ps, wT_sb, wf_ps, wf_sb, late_ld = map(sem, ("wpq_done", "wT_ps", "wT_sb", "wf_ps", "wf_sb", "late_ld"))
        xT_ps, xT_sb, pq_ps, pq_sb = map(sem, ("xT_ps", "xT_sb", "pq_ps", "pq_sb"))
        q_st = sem("q_st")
        node_oh_done, lasts_ps, tile_found = sem("node_oh_done"), sem("lasts_ps"), sem("tile_found")
        tile_rows = [sem(f"tile_rows{k}") for k in range(len(edge_rows))]
        start_done, start_next = sem("start_done"), sem("start_next")
        full_done, full_sum = sem("full_done"), sem("full_sum")
        places_done, hot_done, mid_ps, mid_sb, placed_ps, placed = map(
            sem, ("places_done", "hot_done", "mid_ps", "mid_sb", "placed_ps", "placed"))
        idx_done = sem("idx_done")
        row_ld = [sem(f"row_ld{s}") for s in range(UN)]
        cut_done, win_ps, win_ev = map(sem, ("cut_done", "win_ps", "win_ev"))
        q_ld = [sem(f"q_ld{s}") for s in range(RING)]
        oh_done, m1_done, relu1, z_done, relu2, run_done, t_done, run_ev = map(
            sem, ("oh_done", "m1_done", "relu1", "z_done", "relu2", "run_done", "t_done", "run_ev"))
        run_st = [sem(f"run_st{s}") for s in range(UN)]
        dup_done, move_done = sem("dup_done"), sem("move_done")
        seg_ld = [sem(f"seg_ld{k}") for k in range(NC)]
        x1_sum, var_done, std_done, rstd_done, x1_done = map(
            sem, ("x1_sum", "var_done", "std_done", "rstd_done", "x1_done"))
        res_done, res_st = sem("res_done"), sem("res_st")
        row2_ld = [sem(f"row2_ld{s}") for s in range(UN)]
        sel_done, mt_done, mt_ev, msg_done, msg_ev = map(sem, ("sel_done", "mt_done", "mt_ev", "msg_done", "msg_ev"))
        acc_add = [sem(f"acc_add{k}") for k in range(NACC)]
        acc_ld = [sem(f"acc_ld{c}") for c in range(NC)]
        half_sum, other_half, acc_sum, out_done, out_st = map(sem, ("half_sum", "other_half", "acc_sum", "out_done", "out_st"))

        def grp(i, r, n=UN):
            return n * i + r

        def i_of(i, r, n=UN):
            return n // UN * i + r // UN

        def runs(i, r, n=UN):
            return not isinstance(i, int) or 0 <= n * i + r < G

        def old(i, r, n=UN):
            return not isinstance(i, int) or n * i + r >= 0

        def batch(b):
            return range(b * GT, min(H, (b + 1) * GT))

        node = lambda a: a.rearrange("(h p) d -> p h d", p=P)

        block = ctx.enter_context(nc.Block())

        @block.gpsimd
        def _(pool):
            nc.gpsimd.memset(ident[:], 0.0).then_inc(consts_a, 1)
            nc.gpsimd.memset(shift[:], 0.0).then_inc(consts_a, 1)
            nc.gpsimd.memset(corner[:], 0.0).then_inc(consts_a, 1)
            nc.gpsimd.memset(ones[:], 1.0).then_inc(consts_a, 1)
            nc.gpsimd.memset(eps[:], EPS).then_inc(consts_a, 1)
            kw = dict(allow_small_or_imprecise_dtypes=True)
            nc.gpsimd.iota(chunk_at[:], pattern=[[CN, CH]], base=0, channel_multiplier=0, **kw).then_inc(consts, 1)
            nc.gpsimd.iota(iota_n[:], pattern=[[1, CN]], base=0, channel_multiplier=0, **kw).then_inc(consts, 1)
            nc.gpsimd.iota(lasts[:, TA:TA + 1], pattern=[[0, 1]], base=0, channel_multiplier=TA, **kw).then_inc(consts, 1)
            nc.gpsimd.iota(node_id[:], pattern=[[P, H]], base=0, channel_multiplier=1, **kw).then_inc(consts, 1)
            nc.gpsimd.iota(iota_p[:], pattern=[[0, 1]], base=0, channel_multiplier=1, **kw).then_inc(consts, 1)
            nc.gpsimd.iota(iota_f[:], pattern=[[1, P]], base=0, channel_multiplier=0, **kw).then_inc(consts, 1)
            nc.gpsimd.iota(trash[:], pattern=[[0, 1]], base=NP, channel_multiplier=1, **kw).then_inc(consts, 1)
            pool.wait_ge(consts_a, 5)
            nc.gpsimd.affine_select(out=ident[:], in_=ident[:], compare_op=ALU.not_equal, fill=1.0, base=0,
                                    pattern=[[-1, P]], channel_multiplier=1).then_inc(consts, 1)
            nc.gpsimd.affine_select(out=before[:], in_=ones[:], compare_op=ALU.is_gt, fill=0.0, base=0,
                                    pattern=[[-1, P]], channel_multiplier=1).then_inc(consts, 1)
            nc.gpsimd.affine_select(out=after[:], in_=ones[:], compare_op=ALU.is_gt, fill=0.0, base=0,
                                    pattern=[[1, P]], channel_multiplier=-1).then_inc(consts, 1)
            nc.gpsimd.affine_select(out=shift[:], in_=shift[:], compare_op=ALU.not_equal, fill=1.0, base=-1,
                                    pattern=[[-1, P]], channel_multiplier=1).then_inc(consts, 1)
            nc.gpsimd.affine_select(out=corner[:], in_=corner[:], compare_op=ALU.not_equal, fill=1.0, base=1 - P,
                                    pattern=[[1, P]], channel_multiplier=P).then_inc(consts, 1)
            pool.wait_ge(wt_ld, 16 * WEIGHTS)
            nc.gpsimd.tensor_tensor(wpq[:, 0, :], w2[:, 0, :], w2[:, 1, :], ALU.subtract).then_inc(wpq_done, 1)
            nc.gpsimd.tensor_copy(wpq[:, 1, :], w2[:, 1, :]).then_inc(wpq_done, 1)
            nc.gpsimd.memset(zeros[:], 0.0).then_inc(zeros_set, 1)

            pool.wait_ge(dst_st, 16)
            for c in range(CH):
                k = c % len(edge_rows)
                pool.wait_ge(tile_found, c + 1)
                if c >= len(edge_rows):
                    pool.wait_ge(counted, c - len(edge_rows) + 1)
                for h in range(CH):
                    pool.indirect_dma_start(edge_rows[k][:, h, :], None, dst_tab[:, :],
                                            IOA(ap=tile_i[:, c * CH + h:c * CH + h + 1], axis=0)).then_inc(tile_rows[k], 16)
            pool.wait_ge(q_st, 16 * (HX // GT))

            def gather(i, r):
                pool.wait_ge(idx_done, grp(i, r, RING) + 1)
                if old(i, r - RING, RING):
                    pool.wait_ge(m1_done, grp(i, r - RING, RING) + 1)
                pool.sem_inc(pool_waited, 1)
                for j in range(GT):
                    pool.indirect_dma_start(qg[:, r, j, :], None, q_tab[:, :],
                                            IOA(ap=src_idx[:, r, j:j + 1], axis=0)).then_inc(q_ld[r], 16)

            for r in range(RING):
                gather(0, r)
            with pool.Fori(1, ITR) as i:
                for r in range(RING):
                    gather(i, r)
            for r in range(G - RING * ITR):
                gather(ITR, r)

            for s in range(UN):
                pool.wait_ge(run_st[s], 16 * IT)
            for h in range(H):
                pool.indirect_dma_start(rows[:, h, :], None, seg_tab[:, :],
                                        IOA(ap=end_i[:, h:h + 1], axis=0)).then_inc(seg_ld[chunk_of[h]], 16)
            pool.wait_ge(late_ld, 32)
            for c, cols in enumerate(norm_cols):
                pool.wait_ge(x1_done, c + 1)
                nc.gpsimd.tensor_tensor(res[:, cols, :], x1[:, cols, :], bl_bc[:, :].unsqueeze(1).to_broadcast([P, NORM[c], D]),
                                        ALU.add).then_inc(res_done, 1)

            pool.wait_ge(acc_zero, 16 * (1 + (NACC - 1) * -(-CROWS // ZR)))
            pool.wait_ge(res_st, 16 * NC)

            def scatter(i, r):
                pool.wait_ge(idx_done, G + AHEAD + grp(i, r) + 1)
                pool.wait_ge(msg_ev, grp(i, r) + 1)
                for j in range(GT):
                    if old(i, r - 1):
                        pool.wait_ge(acc_add[j], 16 * grp(i, r))
                    pool.sem_inc(pool_waited, 1)
                    pool.indirect_dma_start(acc_tab[j][:, :], IOA(ap=src_idx[:, r, j:j + 1], axis=0), msg[:, r, j, :], None,
                                            compute_op=ALU.add).then_inc(acc_add[j], 16)

            for r in range(UN):
                scatter(0, r)
            with pool.Fori(1, IT) as i:
                for r in range(UN):
                    scatter(i, r)

            for c, a in enumerate(acc_sb):
                pool.wait_ge(acc_ld[c], 16 * NACC)
                nc.gpsimd.tensor_tensor(a[:, 0], a[:, 0], a[:, 1], ALU.add).then_inc(half_sum, 1)

        @block.sync
        def _(sp):
            ev = lambda a: a[0:(PA - 1) * EPA].rearrange("(p j) -> p j", j=EPA)
            tail = lambda a: a[(PA - 1) * EPA:E].rearrange("(a j) -> a j", a=1)
            cut = 96
            sp.dma_start(dst_i[0:cut, :], ev(dst)[0:cut, :]).then_inc(dst_ld, 16)
            sp.wait_ge(pads_set, 2)
            sp.dma_start(prev_i[1:PA, :], ev(dst)[:, EPA - 1:EPA], allow_slow_non_contiguous=True).then_inc(dst_ld, 16)
            sp.dma_start(dst_i[cut:PA - 1, :], ev(dst)[cut:PA - 1, :]).then_inc(dst_ld, 16)
            sp.dma_start(dst_i[PA - 1:PA, 0:LASTE], tail(dst)).then_inc(dst_ld, 16)
            sp.wait_ge(tabs_ready, 1)
            sp.dma_start(dst_tab.rearrange("(p k) e -> p (k e)", p=PA), dst_f[:, :]).then_inc(dst_st, 16)
            sp.wait_ge(pads_set, 4)
            for a, sbuf, s in ((src, src_i, src_ld), (edge_weight, w_a, w_ld)):
                sp.dma_start(sbuf[0:cut, :], ev(a)[0:cut, :]).then_inc(s, 16)
                sp.dma_start(sbuf[cut:PA - 1, :], ev(a)[cut:PA - 1, :]).then_inc(s, 16)
                sp.dma_start(sbuf[PA - 1:PA, 0:LASTE], tail(a)).then_inc(s, 16)

            sp.wait_ge(tabs_ready, 2)
            sp.dma_start(base_tab.rearrange("a (p k) -> p (a k)", p=PA), base_i[:, :], allow_slow_non_contiguous=True).then_inc(base_ld, 16)
            for a, sbuf in ((seg_row_tab[:, 0, :], rel_u8), (seg_row_tab[:, 1, :], cont_u8), (src_row_tab, src_u16)):
                sp.dma_start(a.rearrange("(p q) e -> p q e", p=PA),
                             sbuf[:, :].rearrange("p (q e) -> p q e", e=GE)).then_inc(tabs_st, 16)
            sp.wait_ge(base_ld, 16)
            sp.dma_start(base_row[:, :], base_tab[:, :]).then_inc(base_ld, 16)
            for k in range(HX // GT):
                sp.wait_ge(pq_sb, 2 * k + 2)
                b = min(H, (k + 1) * GT)
                sp.dma_start(node(q_tab[k * GT * P:b * P, :]), q_sb[:, k * GT:b, :]).then_inc(q_st, 16)
            sp.wait_ge(tabs_st, 48)

            def rows0(i, r):
                sp.dma_start(row_bc[:, r, :], seg_row_tab.rearrange("g a e -> g (a e)")[ds(grp(i, r), 1), :]
                             .to_broadcast([P, 2 * GE])).then_inc(row_ld[r], 16)

            def rows1(i, r):
                sp.dma_start(row_bc[:, r, :].bitcast(U16), src_row_tab[ds(grp(i, r), 1), :].to_broadcast([P, GE])).then_inc(row2_ld[r], 16)

            sp.wait_ge(counted, CH)
            for r in range(UN):
                rows0(0, r)

            def store(i, r):
                sp.wait_ge(run_ev, grp(i, r) + 1)
                sp.sem_inc(sp_waited, 1)
                sp.dma_start(seg_tab.rearrange("(g t e) d -> g e t d", e=P, t=GT)[ds(grp(i, r), 1)].rearrange("a e t d -> (a e) t d"),
                             run_e[:, r % UN, :, :]).then_inc(run_st[r % UN], 16)

            with sp.Fori(0, IT - 1) as i:
                for r in range(UN):
                    sp.wait_ge(run_done, grp(i, r) + 1)
                    sp.sem_inc(sp_waited, 1)
                    rows0(i + 1, r)
                    store(i, r)
            for r in range(UN):
                store(IT - 1, r)

            sp.wait_ge(run_done, G)
            for r in range(UN):
                rows1(0, r)

            spans = [(acc_tab[0], NP, P)] + [(acc_tab[k], a, min(ZR, CROWS - a)) for k in range(1, NACC) for a in range(0, CROWS, ZR)]
            sp.wait_ge(zeros_set, 1)
            for c in range(NC):
                sp.wait_ge(seg_ld[c], 16 * NORM[c])
                for tab, a, n in spans[c::NC]:
                    sp.dma_start(tab[a:a + n, :].rearrange("(p q) d -> p (q d)", p=P), zeros[:, 0:n // P * D]).then_inc(acc_zero, 16)
            for c, cols in enumerate(norm_cols):
                sp.wait_ge(res_done, c + 1)
                sp.dma_start(node(acc_tab[0][0:NP, :])[:, cols, :], res[:, cols, :]).then_inc(res_st, 16)

            with sp.Fori(1, IT) as i:
                for r in range(UN):
                    sp.wait_ge(dup_done, grp(i, r - UN) + 1)
                    sp.sem_inc(sp_waited, 1)
                    rows1(i, r)

            for c, cols in enumerate(norm_cols):
                for k in range(NACC):
                    if c == 0:
                        sp.wait_ge(acc_add[k], 16 * G)
                    sp.dma_start(acc_sb[c][:, k], node(acc_tab[k][0:NP, :])[:, cols, :]).then_inc(acc_ld[c], 16)
            for c, cols in enumerate(norm_cols):
                sp.wait_ge(out_done, c + 1)
                end = min(cols.stop, H - 1)
                sp.dma_start(node(out[cols.start * P:end * P, :]), acc_sb[c][:, 0, 0:end - cols.start, :]).then_inc(out_st, 16)
            sp.dma_start(out[(H - 1) * P:N, :], acc_sb[-1][0:LASTN, 0, NORM[-1] - 1, :]).then_inc(out_st, 16)
            sp.wait_ge(out_st, 16 * (NC + 1))

        @block.scalar
        def _(act):
            def load_x(k):
                act.dma_start(x_sb[:, k * XL:(k + 1) * XL, :], node(x[k * XL * P:(k + 1) * XL * P, :])).then_inc(x_ld[k], 16)

            for sbuf, a in ((w1[:], W1), (w2[:], W2.rearrange("(k p) d -> p k d", p=P)), (wl[:], WL)):
                act.dma_start(sbuf, a).then_inc(wt_ld, 16)
            load_x(0)
            for k, a in enumerate((b1, b2, b3)):
                act.dma_start(bias[:, k:k + 1], a.rearrange("(p a) -> p a", a=1)).then_inc(wt_ld, 16)
            act.wait_ge(dst_st, 16)
            for k in range(1, len(x_ld) - 1):
                load_x(k)
            act.wait_ge(pads_set, 5)
            act.dma_start(x_sb[0:LASTN, H - 1, :], x[(H - 1) * P:N, :]).then_inc(x_ld[-1], 16)

            act.dma_start(w3[:], W3).then_inc(late_ld, 16)
            act.dma_start(bl_bc[:], bL.rearrange("(a d) -> a d", a=1).to_broadcast([P, D])).then_inc(late_ld, 16)

            act.wait_ge(wT_ps, 2)
            nc.scalar.activation(wT[:, :, :], z_ps[:, 0, 0:2 * D].rearrange("p (k d) -> p k d", d=D), ACT.Copy).then_inc(wT_sb, 1)
            act.wait_ge(wf_ps, 1)
            nc.scalar.activation(wf[:, :, :], z_ps[:, 1, 0:2 * D].rearrange("p (k d) -> p k d", d=D), ACT.Copy).then_inc(wf_sb, 1)
            nc.scalar.activation(bias12[:], z_ps[:, 1, 2 * D:2 * D + 1], ACT.Identity, bias=bias[:, 1:2]).then_inc(wf_sb, 1)

            def xT_copy(k):
                act.wait_ge(xT_ps, k + 1)
                if k >= 2:
                    act.wait_ge(pq_ps, 2 * (k - 1))
                nc.scalar.activation(xT[:, k % 2, :], m1_ps[:, k % 2, :], ACT.Copy).then_inc(xT_sb, 1)

            def pq_copy(k):
                for a, to in enumerate((p_sb, q_sb)):
                    act.wait_ge(pq_ps, 2 * k + a + 1)
                    nc.scalar.activation(to[:, k * GT:(k + 1) * GT, :], by_block(pq_banks[k % 2][:, a, :]), ACT.Copy).then_inc(pq_sb, 1)

            for k in range(HX // GT + 1):
                if k < HX // GT:
                    xT_copy(k)
                if k >= 1:
                    pq_copy(k - 1)

            def place(stage, b):
                banks = place_ps if stage == 0 else place_ps[2:]
                _, offs = nc.values_load_multi_w_load_instructions(
                    col_off_i[0:1, b * GT:(b + 1) * GT], engines=bass.OrderedEngineSet([mybir.EngineType.Activation]), min_val=0, max_val=NP,
                    skip_runtime_bounds_check_because="a count of full nodes in the columns before is below the count of nodes")
                act.wait_ge(placed_ps, stage * NB + b + 1)
                for j, h in enumerate(batch(b)):
                    if stage * H + h > 0:
                        act.wait_ge(placed, stage * H + h)
                    nc.scalar.activation(compact_T[stage][:, ds(offs[j], P)], banks[b % len(banks)][:, j * P:(j + 1) * P],
                                         ACT.Copy).then_inc(placed, 1)

            def cut(layer, i, r):
                _, base = nc.values_load_multi_w_load_instructions(
                    base_row[0:1, ds(GT * grp(i, r), GT)], engines=bass.OrderedEngineSet([mybir.EngineType.Activation]), min_val=0, max_val=NP,
                    skip_runtime_bounds_check_because="a count of segments opened before a tile is below the count of nodes")
                if old(i, r - 2):
                    act.wait_ge(win_ps, layer * G + grp(i, r - 2) + 1)
                for j in range(GT):
                    nc.scalar.activation(win_cols[:, r % 2, j * P:(j + 1) * P], compact_T[layer][:, ds(base[j], P)], ACT.Copy).then_inc(cut_done, 1)

            act.wait_ge(q_st, 16 * (HX // GT))
            for b in range(NB):
                act.wait_ge(places_done, 1 + (batch(b)[0] >= SPLIT * CH))
                place(0, b)
            act.wait_ge(placed, H)
            act.wait_ge(base_ld, 32)

            def relu_1(i, r):
                s = r % 2
                act.wait_ge(m1_done, grp(i, r) + 1)
                if old(i, r - 2):
                    act.wait_ge(z_done, grp(i, r - 2) + 1)
                nc.scalar.activation(m1[:, s, :], m1_ps[:, s, :], ACT.Relu, bias=bias12[:]).then_inc(relu1, 1)

            def relu_2(i, r):
                s = r % 2
                act.wait_ge(z_done, grp(i, r) + 1)
                if old(i, r - 2):
                    act.wait_ge(run_done, grp(i, r - 2) + 1)
                nc.scalar.activation(m2[:, s, :], z_ps[:, s, :], ACT.Relu, bias=bias[:, 2:3]).then_inc(relu2, 1)

            def run_copy(i, r):
                act.wait_ge(t_done, grp(i, r) + 1)
                if old(i, r - UN):
                    act.wait_ge(run_st[r % UN], 16 * i_of(i, r))
                nc.scalar.activation(run_e[:, r % UN, :, :], t_ps[:, r % 2, :].rearrange("p (t d) -> p t d", d=D), ACT.Copy).then_inc(run_ev, 1)

            def step0(i, r):
                if runs(i, r):
                    cut(0, i, r)
                for part, lag in ((relu_1, 2), (relu_2, 3), (run_copy, 4)):
                    if runs(i, r - lag):
                        part(i, r - lag)

            for r in range(UN):
                step0(0, r)
            with act.Fori(1, IT) as i:
                for r in range(UN):
                    step0(i, r)
            for r in range(4):
                step0(IT, r)

            def roots(n, c):
                act.wait_ge(var_done, n * NC + c + 1)
                cols = norm_cols[c]
                nc.scalar.activation(std[:, cols], mv[:, cols, 1], ACT.Sqrt, bias=eps[:]).then_inc(std_done, 1)

            def middle(b):
                act.wait_ge(mid_ps, b + 1)
                if b >= 2:
                    act.wait_ge(placed_ps, NB + b - 1)
                w = len(batch(b)) * P
                nc.scalar.activation(m1[:, b % 2, 0:w], m1_ps[:, b % 2, 0:w], ACT.Copy).then_inc(mid_sb, 1)

            roots(0, 0)
            for c in range(NC):
                last = [b for b in range(NB) if chunk_of[batch(b)[-1]] == c]
                for b in last:
                    middle(b)
                    if b == last[0] and c + 1 < NC:
                        roots(0, c + 1)
                    if b >= 1:
                        place(1, b - 1)
            place(1, NB - 1)

            def mix_ev(i, r):
                s = r % 2
                act.wait_ge(mt_done, grp(i, r) + 1)
                if old(i, r - 2):
                    act.wait_ge(msg_done, grp(i, r - 2) + 1)
                nc.scalar.activation(m1[:, s, :], m1_ps[:, s, :], ACT.Copy).then_inc(mt_ev, 1)

            def window_ev(i, r):
                act.wait_ge(win_ps, G + grp(i, r) + 1)
                if old(i, r - UN):
                    act.wait_ge(msg_done, grp(i, r - UN) + 1)
                nc.scalar.activation(win[:, r, :, :], by_block(s_ps[:, r % 2, :]), ACT.Copy).then_inc(win_ev, 1)

            def message_ev(i, r):
                s = r % 2
                act.wait_ge(msg_done, grp(i, r) + 1)
                if old(i, r - UN):
                    for k in range(NACC):
                        act.wait_ge(acc_add[k], 16 * (grp(i, r - UN) + 1))
                nc.scalar.activation(msg[:, r % UN, :, :], z_ps[:, s, :].rearrange("p (t d) -> p t d", d=D), ACT.Copy).then_inc(msg_ev, 1)

            def step1(i, r):
                if runs(i, r):
                    cut(1, i, r)
                    mix_ev(i, r)
                if runs(i, r - 1):
                    message_ev(i, r - 1)
                if runs(i, r):
                    window_ev(i, r)

            act.wait_ge(placed, 2 * H)
            cut(1, 0, 0)
            mix_ev(0, 0)
            window_ev(0, 0)
            message_ev(0, 0)
            cut(1, 0, 1)
            mix_ev(0, 1)
            window_ev(0, 1)
            for r in range(2, UN):
                step1(0, r)
            with act.Fori(1, IT) as i:
                for r in range(UN):
                    step1(i, r)
            step1(IT, 0)

            for c, cols in enumerate(norm_cols):
                roots(1, c)
                act.wait_ge(rstd_done, NC + c + 1)
                for h in range(NORM[c]):
                    k = cols.start + h
                    last = nc.scalar.activation(acc_sb[c][:, 0, h, :], acc_sb[c][:, 0, h, :], ACT.Identity, bias=shift_by[:, k:k + 1], scale=rstd[:, k:k + 1])
                last.then_inc(out_done, 1)

        @block.vector
        def _(dve):
            chain = [0]

            def link(ins):
                chain[0] += 1
                ins.then_inc(dve_own, 1)
                dve.wait_ge(dve_own, chain[0])

            V = nc.vector
            V.memset(prev_i[:], -1).then_inc(pads_set, 1)
            V.memset(dst_i[96:PA, LASTE:], N).then_inc(pads_set, 1)
            V.memset(src_i[96:PA, LASTE:], N).then_inc(pads_set, 1)
            V.memset(w_a[96:PA, LASTE:], 0.0).then_inc(pads_set, 1)
            V.memset(x_sb[:, H - 1:HX, :], 0.0).then_inc(pads_set, 1)
            V.memset(src_ti[:, T:], 0)
            V.memset(col_off_i[:, H:], 0)
            link(V.memset(start[:, H:H + 1], 0.0))

            dve.wait_ge(dst_ld, 64)
            V.tensor_copy(dst_f[:], dst_i[:]).then_inc(tabs_ready, 1)
            dve.wait_ge(tabs_ready, 1)
            link(V.tensor_copy(prev_f[:], prev_i[:]))
            dve.wait_ge(consts, CONSTS)
            V.tensor_copy(lasts[:, 0:TA], dst_f[:, :].rearrange("p (k e) -> p k e", e=P)[:, :, P - 1])
            V.tensor_scalar(prev_c[:], chunk_at[0:PA, :], -1.0, prev_f[:], ALU.mult, ALU.add)
            link(V.tensor_scalar(last_c[:], chunk_at[0:PA, :], -1.0, dst_f[:, EPA - 1:EPA], ALU.mult, ALU.add))

            def node_partition(c):
                s = c % 2
                if c >= 2:
                    dve.wait_ge(lasts_ps, c - 1)
                link(V.tensor_scalar(above[0:PA, s, 0:CN], iota_n[0:PA, :], prev_c[:, c:c + 1], None, ALU.is_gt))
                V.scalar_tensor_tensor(node_oh[0:PA, s, 0:CN], iota_n[0:PA, :], last_c[:, c:c + 1], above[0:PA, s, 0:CN],
                                       ALU.is_le, ALU.mult).then_inc(node_oh_done, 1)

            def node_tile(c):
                cols = slice(c * CH, (c + 1) * CH)
                less = tile_less[:, c % 2, :, :]
                dve.wait_ge(lasts_ps, c + 1)
                found = lasts_v(c)
                link(V.tensor_tensor(less, found[:, :, 0:TA], node_id[:, cols].unsqueeze(2).to_broadcast([P, CH, TA]), ALU.is_lt))
                link(V.tensor_reduce(tile_in[:, cols], less, axis=AX_X, op=ALU.add))
                link(V.tensor_tensor(tile_of[:, cols], tile_in[:, cols], found[:, :, TA], ALU.add))
                V.tensor_copy(tile_i[:, cols], tile_of[:, cols]).then_inc(tile_found, 1)

            for c in range(CH + 1):
                if c < CH:
                    node_partition(c)
                if c >= 1:
                    node_tile(c - 1)

            V.tensor_tensor(cont[:, 1:], dst_f[:, 1:], dst_f[:, :EPA - 1], ALU.is_equal)
            link(V.tensor_tensor(cont[:, 0:1], dst_f[:, 0:1], prev_f[:], ALU.is_equal))
            V.tensor_copy(cont_u8[:], cont[:])
            link(V.tensor_scalar(opens[:], cont[:], -1.0, 1.0, ALU.mult, ALU.add))
            V.tensor_tensor_scan(cid[:], opens[:], opens[:], 0.0, ALU.add, ALU.max).then_inc(opens_done, 1)
            dve.wait_ge(src_ld, 48)
            V.tensor_copy(src_f[:], src_i[:]).then_inc(src_ready, 1)
            V.tensor_copy(src_u16[:], src_i[:])
            dve.wait_ge(cid_sum, 1)
            link(V.tensor_scalar(cid_off[:], s_ps[0:PA, 0, 0:1], -1.0, None, ALU.add))
            link(V.tensor_scalar(cid[:], cid[:], cid_off[:], None, ALU.add))
            cidv = cid[:, :].rearrange("p (k e) -> p k e", e=P)
            V.tensor_copy(base_i[:], cidv[:, :, 0])
            link(V.tensor_copy(base_f[:], cidv[:, :, 0]))
            link(V.tensor_tensor(rel[:, :].rearrange("p (k e) -> p k e", e=P), cidv,
                                 base_f[:, :].unsqueeze(2).to_broadcast([PA, TA, P]), ALU.subtract))
            V.tensor_copy(rel_u8[:], rel[:]).then_inc(tabs_ready, 1)

            def count(c):
                k = c % len(edge_rows)
                dve.wait_ge(tile_rows[k], 16 * CH * (c // len(edge_rows) + 1))
                if c >= 2:
                    dve.wait_ge(counted, c - 1)
                for h in range(CH):
                    n = c * CH + h
                    last = V.tensor_scalar(above[:, c % 2, h * P:(h + 1) * P], edge_rows[k][:, h, :], node_id[:, n:n + 1], None,
                                           ALU.is_lt, ALU.add, accum_out=below[:, n:n + 1])
                last.then_inc(counted, 1)

            def places(n, a, b, known):
                new = slice((0, SPLIT * CH + CH)[n], known)
                cols = slice(a, b)
                dve.wait_ge(counted, -(-known // CH))
                V.scalar_tensor_tensor(start[:, new], tile_of[:, new], float(P), below[:, new], ALU.mult, ALU.add).then_inc(start_done, 1)
                dve.wait_ge(start_next, n + 1)
                V.tensor_tensor(full[:, cols], end_ps[:, cols], start[:, cols], ALU.is_gt).then_inc(full_done, 1)
                V.tensor_scalar(end_i[:, cols], end_ps[:, cols], -1.0, 0.0, ALU.add, ALU.max)
                dve.wait_ge(full_sum, n + 1)
                link(V.tensor_copy(col_full[:, cols], col_full_ps[:, cols]))
                link(V.tensor_tensor_scan(col_off[:, cols], col_full[:, cols], col_full[:, cols], col_off[:, a - 1:a] if a else 0.0, ALU.add, ALU.max))
                V.tensor_tensor(col_off_i[:, cols], col_off[:, cols], col_full[:, cols], ALU.subtract)
                link(V.scalar_tensor_tensor(in_col[:, cols], in_col_ps[:, cols], 1.0, full[:, cols], ALU.add, ALU.mult))
                V.tensor_scalar(in_col[:, cols], in_col[:, cols], -1.0, None, ALU.add).then_inc(places_done, 1)
                dve.wait_ge(places_done, n + 1)

            def one_hots(columns):
                for h in columns:
                    V.tensor_scalar(hot[h], iota_f[:], in_col[:, h:h + 1], None, ALU.is_equal).then_inc(hot_done, 1)

            def by_tile(n, outs):
                dve.wait_ge(tr_out, n + 1)
                for a in range(2):
                    for o in outs:
                        last = V.tensor_copy(o.rearrange("p (q k) -> p k q", k=TA)[:, 4 * a:4 * a + 4, :],
                                             tile_ps[n][:, a, :].rearrange("p (b q) -> p b q", q=P)[:, :, 0:PA])
                last.then_inc(tr_copied, 1)

            def indices(i, r):
                V.tensor_copy(src_idx[:, r % RING, :], src_ti[:, ds(GT * grp(i, r, RING), GT)]).then_inc(idx_done, 1)

            for c in range(SPLIT + 1):
                if c == SPLIT:
                    by_tile(0, [src_t[:, :], src_ti[:, 0:T]])
                    dve.wait_ge(tr_copied, 1)
                    for r in range(RING):
                        indices(0, r)
                count(c)
            places(0, 0, SPLIT * CH, (SPLIT + 1) * CH)
            one_hots(range(SPLIT * CH))
            for c in range(SPLIT + 1, CH):
                count(c)
            places(1, SPLIT * CH, H, H)
            one_hots(range(SPLIT * CH, H))

            def one_hot(i, r):
                s = r % 2
                dve.wait_ge(row_ld[r % UN], 16 * (i_of(i, r, RING) + 1))
                if old(i, r - 2, RING):
                    dve.wait_ge(m1_done, grp(i, r - 2, RING) + 1)
                V.tensor_scalar(oh[:, s, :], row_bc[:, r % UN, 0:GE], iota_p[:], None, ALU.is_equal).then_inc(oh_done, 1)

            def window_ev(i, r):
                dve.wait_ge(win_ps, grp(i, r, RING) + 1)
                if old(i, r - UN, RING):
                    dve.wait_ge(m1_done, grp(i, r - UN, RING) + 1)
                V.tensor_copy(win[:, r % UN, :, :], by_block(s_ps[:, r % 2, :])).then_inc(win_ev, 1)

            def scan(i, r):
                s = r % 2
                dve.wait_ge(relu2, grp(i, r, RING) + 1)
                if old(i, r - 2, RING):
                    dve.wait_ge(t_done, grp(i, r - 2, RING) + 1)
                first = 0.0
                if old(i, r - 1, RING):
                    dve.wait_ge(run_done, grp(i, r, RING))
                    first = run[:, 1 - s, GE - 1:GE]
                V.tensor_tensor_scan(run[:, s, :], row_bc[:, r % UN, GE:2 * GE], m2[:, s, :], first, ALU.mult, ALU.max).then_inc(run_done, 1)

            def step0(i, r):
                if runs(i, r - 2, RING):
                    if old(i, r - 3, RING):
                        dve.wait_ge(q_ld[(r - 3) % RING], 16 * GT * (i + (r - 3) // RING + 1))
                        indices(i, r - 2 + AHEAD)
                if runs(i, r - 1, RING):
                    one_hot(i, r - 1)
                if runs(i, r - 4, RING):
                    scan(i, r - 4)
                if runs(i, r - 1, RING):
                    window_ev(i, r - 1)

            by_tile(1, [w_t[:, :]])
            by_tile(2, [rel_t[:, :]])
            V.tensor_scalar(to_trash[:], src_t[:], -1.0, trash[:], ALU.mult, ALU.add)
            for r in range(RING):
                step0(0, r)
            with dve.Fori(1, ITR) as i:
                for r in range(RING):
                    step0(i, r)
            for r in range(G - RING * ITR + 4):
                step0(ITR, r)

            def moments(c, v):
                for h in range(NORM[c]):
                    last = V.bn_stats(part[:, h, :], v[:, h, :])
                link(last)
                for h in range(NORM[c]):
                    last = V.bn_aggr(mv[:, norm_cols[c].start + h, :], part[:, h, :])
                last.then_inc(var_done, 1)

            def scales(n, c):
                cols = norm_cols[c]
                dve.wait_ge(std_done, n * NC + c + 1)
                link(V.reciprocal(rstd[:, cols], std[:, cols]))
                V.scalar_tensor_tensor(shift_by[:, cols], mv[:, cols, 0], -1.0, rstd[:, cols], ALU.mult, ALU.mult).then_inc(rstd_done, 1)

            dve.wait_ge(m1_done, G)
            dve.wait_ge(t_done, G)
            one_hots(range(min(H, hot_late)))
            for k in range(UN):
                dve.wait_ge(run_st[k], 16 * IT)
            one_hots(range(hot_late, H))
            for c, cols in enumerate(norm_cols):
                dve.wait_ge(seg_ld[c], 16 * NORM[c])
                for h in range(cols.start, cols.stop):
                    last = V.scalar_tensor_tensor(x1[:, h, :], rows[:, h, :], full[:, h:h + 1], x_sb[:, h, :], ALU.mult, ALU.add)
                last.then_inc(x1_sum, 1)
                dve.wait_ge(x1_sum, c + 1)
                moments(c, x1[:, cols, :])
                scales(0, c)
                dve.wait_ge(rstd_done, c + 1)
                for h in range(cols.start, cols.stop):
                    last = V.tensor_scalar(x1[:, h, :], x1[:, h, :], rstd[:, h:h + 1], shift_by[:, h:h + 1], ALU.mult, ALU.add)
                last.then_inc(x1_done, 1)

            def selections(i, r):
                s = r % 2
                dve.wait_ge(row2_ld[r], 16 * (i + 1))
                if old(i, r - 2):
                    dve.wait_ge(mt_done, grp(i, r - 2) + 1)
                V.tensor_tensor(oh[:, s, :].rearrange("p (t c) -> p t c", c=P), iota_f[:, :].unsqueeze(1).to_broadcast([P, GT, P]),
                                rel_t[:, ds(GT * grp(i, r), GT)].unsqueeze(2).to_broadcast([P, GT, P]), ALU.is_equal)
                src16 = row_bc[:, r, :].bitcast(U16)
                tile_src = lambda j: (src16[:, j * P:(j + 1) * P], src_t[:, ds(GT * grp(i, r) + j, 1)])
                for j in range(GT):
                    row, col = tile_src(j)
                    last = V.tensor_scalar(sel[:, s, j * P:(j + 1) * P], row, col, w_t[:, ds(GT * grp(i, r) + j, 1)], ALU.is_equal, ALU.mult)
                last.then_inc(sel_done, 1)
                if old(i, r - 1):
                    dve.wait_ge(idx_done, G + AHEAD + grp(i, r))
                for j in range(GT):
                    row, col = tile_src(j)
                    last = V.scalar_tensor_tensor(junk[:, j, :], row, col, before[:], ALU.is_equal, ALU.mult, accum_out=dup[:, j:j + 1])
                last.then_inc(dup_done, 1)

            def accumulator_rows(i, r):
                dve.wait_ge(dup_done, grp(i, r) + 1)
                V.scalar_tensor_tensor(move[:], dup[:], 0.5, to_trash[:, ds(GT * grp(i, r), GT)], ALU.is_gt, ALU.mult).then_inc(move_done, 1)
                if old(i, r - UN):
                    for k in range(NACC):
                        dve.wait_ge(acc_add[k], 16 * (grp(i, r - UN) + 1))
                dve.wait_ge(move_done, grp(i, r) + 1)
                V.tensor_tensor(src_idx[:, r, :], move[:], src_t[:, ds(GT * grp(i, r), GT)], ALU.add).then_inc(idx_done, 1)

            def step1(i, r):
                selections(i, r)
                accumulator_rows(i, r)

            dve.wait_ge(mid_ps, NB)
            for r in range(UN):
                step1(0, r)
            with dve.Fori(1, IT) as i:
                for r in range(UN):
                    step1(i, r)

            for c in range(NC + 1):
                if c < NC:
                    a = acc_sb[c]
                    dve.wait_ge(acc_ld[c], 16 * NACC)
                    V.tensor_tensor(a[:, 2], a[:, 2], a[:, 3], ALU.add).then_inc(other_half, 1)
                if c >= 1:
                    scales(1, c - 1)
                if c < NC:
                    dve.wait_ge(half_sum, c + 1)
                    dve.wait_ge(other_half, c + 1)
                    V.tensor_tensor(a[:, 0], a[:, 0], a[:, 2], ALU.add).then_inc(acc_sum, 1)
                    dve.wait_ge(acc_sum, c + 1)
                    moments(c, a[:, 0])

        @block.tensor
        def _(pe):
            mm = nc.tensor.matmul
            pe.wait_ge(consts, CONSTS)

            def node_lasts(c):
                pe.wait_ge(node_oh_done, c + 1)
                if c >= 2:
                    pe.wait_ge(tile_found, c - 1)
                for h in range(CH):
                    last = mm(lasts_v(c)[:, h, :], lhsT=node_oh[0:PA, c % 2, h * P:(h + 1) * P], rhs=lasts[:], start=True, stop=True)
                last.then_inc(lasts_ps, 1)

            def x_transposed(k):
                if k * GT % XL == 0:
                    pe.wait_ge(x_ld[k * GT // XL], 16)
                if k >= 2:
                    pe.wait_ge(xT_sb, k - 1)
                for j in range(GT):
                    last = nc.tensor.transpose(m1_ps[:, k % 2, j * P:(j + 1) * P], x_sb[:, k * GT + j, :], ident[:])
                last.then_inc(xT_ps, 1)

            def p_and_q(k):
                pe.wait_ge(xT_sb, k + 1)
                for a in range(2):
                    if k >= 2:
                        pe.wait_ge(pq_sb, 2 * (k - 2) + a + 1)
                    for j in range(GT):
                        last = mm(pq_banks[k % 2][:, a, j * D:(j + 1) * D], lhsT=xT[:, k % 2, j * P:(j + 1) * P], rhs=wf[:, a, :],
                                  start=True, stop=True)
                    last.then_inc(pq_ps, 1)

            def by_tile(n, a):
                for k in range(TA):
                    last = nc.tensor.transpose(tile_ps[n][:, k // GT, k % GT * P:k % GT * P + PA], a[:, k * P:(k + 1) * P], ident[0:PA, 0:PA])
                last.then_inc(tr_out, 1)

            node_lasts(0)
            node_lasts(1)
            pe.wait_ge(wt_ld, 16 * WEIGHTS)
            nc.tensor.transpose(z_ps[:, 0, 0:D], w1[:], ident[:]).then_inc(wT_ps, 1)
            nc.tensor.transpose(z_ps[:, 0, D:2 * D], wl[:], ident[:]).then_inc(wT_ps, 1)
            pe.wait_ge(wpq_done, 2)
            pe.wait_ge(wT_sb, 1)
            mm(z_ps[:, 1, 0:2 * D], lhsT=wT[:, 0, :], rhs=wpq[:, :, :].rearrange("p k d -> p (k d)"), start=True, stop=True)
            mm(z_ps[:, 1, 2 * D:2 * D + 1], lhsT=w2[:, 0, :], rhs=bias[:, 0:1], start=True, stop=True).then_inc(wf_ps, 1)
            for k in range(HX // GT + 1):
                for c in (2 * k, 2 * k + 1):
                    if 2 <= c < CH:
                        node_lasts(c)
                if k == 5:
                    pe.wait_ge(opens_done, 1)
                    pe.wait_ge(tile_found, CH)
                    mm(s_ps[0:PA, 0, 0:1], lhsT=after[0:PA, 0:PA], rhs=cid[:, EPA - 1:EPA], start=True, stop=True).then_inc(cid_sum, 1)
                if k == 8:
                    pe.wait_ge(src_ready, 1)
                    pe.wait_ge(tabs_ready, 2)
                    by_tile(0, src_f)
                if k < HX // GT:
                    x_transposed(k)
                if k == 1:
                    pe.wait_ge(wf_sb, 2)
                if k >= 1:
                    p_and_q(k - 1)
            pe.wait_ge(pq_sb, 2 * (HX // GT))
            def places(n, a, b):
                pe.wait_ge(start_done, n + 1)
                mm(end_ps[:, a:b], lhsT=shift[:], rhs=start[:, a:b], start=True, stop=False)
                mm(end_ps[:, a:b], lhsT=corner[:], rhs=start[:, a + 1:b + 1], start=False, stop=True).then_inc(start_next, 1)
                pe.wait_ge(full_done, n + 1)
                mm(in_col_ps[:, a:b], lhsT=after[:], rhs=full[:, a:b], start=True, stop=True)
                mm(col_full_ps[:, a:b], lhsT=ones[:], rhs=full[:, a:b], start=True, stop=True).then_inc(full_sum, 1)

            def place(stage, b, banks):
                src = (p_sb, x1)[stage]
                pe.wait_ge(hot_done, stage * H + batch(b)[-1] + 1)
                for j, h in enumerate(batch(b)):
                    last = mm(banks[b % len(banks)][:, j * P:(j + 1) * P], lhsT=src[:, h, :], rhs=hot[h], start=True, stop=True)
                return last

            pe.wait_ge(tr_copied, 1)
            places(0, 0, SPLIT * CH)
            for b in range(NB):
                if b * GT == SPLIT * CH:
                    pe.wait_ge(places_done, 1)
                    places(1, SPLIT * CH, H)
                if b >= len(place_ps):
                    pe.wait_ge(placed, (b - len(place_ps) + 1) * GT)
                place(0, b, place_ps).then_inc(placed_ps, 1)
            pe.wait_ge(w_ld, 48)
            by_tile(1, w_a)
            by_tile(2, rel)

            def window(i, r, layer=0, n=RING):
                s = r % 2
                pe.wait_ge(cut_done, GT * (layer * G + grp(i, r, n) + 1))
                if old(i, r - 2, n):
                    pe.wait_ge(win_ev, layer * G + grp(i, r - 2, n) + 1)
                for j in range(GT):
                    last = nc.tensor.transpose(s_ps[:, s, j * P:(j + 1) * P], win_cols[:, s, j * P:(j + 1) * P], ident[:])
                last.then_inc(win_ps, 1)

            def gathered(i, r):
                s = r % 2
                pe.wait_ge(q_ld[r % RING], 16 * GT * (i + r // RING + 1))
                pe.wait_ge(win_ev, grp(i, r, RING) + 1)
                pe.wait_ge(oh_done, grp(i, r, RING) + 1)
                if old(i, r - 2, RING):
                    pe.wait_ge(relu1, grp(i, r - 2, RING) + 1)
                for j in range(GT):
                    c = slice(j * P, (j + 1) * P)
                    mm(m1_ps[:, s, c], lhsT=qg[:, r % RING, j, :], rhs=ident[:], start=True, stop=False)
                    last = mm(m1_ps[:, s, c], lhsT=win[:, r % UN, j, :], rhs=oh[:, s, c], start=False, stop=True)
                last.then_inc(m1_done, 1)

            pe.wait_ge(late_ld, 32)
            pe.wait_ge(placed, H)
            pe.wait_ge(tr_copied, 3)

            def second(i, r):
                s = r % 2
                pe.wait_ge(relu1, grp(i, r, RING) + 1)
                if old(i, r - 2, RING):
                    pe.wait_ge(relu2, grp(i, r - 2, RING) + 1)
                mm(z_ps[:, s, :], lhsT=w3[:], rhs=m1[:, s, :], start=True, stop=True).then_inc(z_done, 1)

            def by_edge(i, r):
                s = r % 2
                pe.wait_ge(run_done, grp(i, r, RING) + 1)
                if old(i, r - 2, RING):
                    pe.wait_ge(run_ev, grp(i, r - 2, RING) + 1)
                for j in range(GT):
                    c = slice(j * P, (j + 1) * P)
                    last = nc.tensor.transpose(t_ps[:, s, c], run[:, s, c], ident[:])
                last.then_inc(t_done, 1)

            def step0(i, r):
                for part, lag in ((gathered, 2), (window, 1), (second, 3), (by_edge, 4)):
                    if runs(i, r - lag, RING):
                        part(i, r - lag)

            for r in range(RING):
                step0(0, r)
            with pe.Fori(1, ITR) as i:
                for r in range(RING):
                    step0(i, r)
            for r in range(G - RING * ITR + 4):
                step0(ITR, r)

            def product(b):
                pe.wait_ge(mid_sb, b + 1)
                if b >= 2:
                    pe.wait_ge(placed, H + (b - 1) * GT)
                w = len(batch(b)) * P
                mm(place_ps[2 + b % 2][:, 0:w], lhsT=wlT[:], rhs=m1[:, b % 2, 0:w], start=True, stop=True).then_inc(placed_ps, 1)

            for b in range(NB):
                pe.wait_ge(x1_done, chunk_of[batch(b)[-1]] + 1)
                if b >= 2:
                    pe.wait_ge(mid_sb, b - 1)
                place(1, b, place_ps[0:2]).then_inc(mid_ps, 1)
                if b >= 1:
                    product(b - 1)
            product(NB - 1)

            def mix(i, r):
                s = r % 2
                pe.wait_ge(sel_done, grp(i, r) + 1)
                if old(i, r - 2):
                    pe.wait_ge(mt_ev, grp(i, r - 2) + 1)
                for j in range(GT):
                    c = slice(j * P, (j + 1) * P)
                    last = mm(m1_ps[:, s, c], lhsT=oh[:, s, c], rhs=sel[:, s, c], start=True, stop=True)
                last.then_inc(mt_done, 1)

            def message(i, r):
                s = r % 2
                pe.wait_ge(mt_ev, grp(i, r) + 1)
                pe.wait_ge(win_ev, G + grp(i, r) + 1)
                if old(i, r - 2):
                    pe.wait_ge(msg_ev, grp(i, r - 2) + 1)
                for j in range(GT):
                    c = slice(j * P, (j + 1) * P)
                    last = mm(z_ps[:, s, c], lhsT=m1[:, s, c], rhs=win[:, r % UN, j, :], start=True, stop=True)
                last.then_inc(msg_done, 1)

            def step1(i, r):
                if runs(i, r):
                    mix(i, r)
                    window(i, r, 1, UN)
                if runs(i, r - 1):
                    message(i, r - 1)

            mix(0, 0)
            window(0, 0, 1, UN)
            mix(0, 1)
            message(0, 0)
            window(0, 1, 1, UN)
            for r in range(2, UN):
                step1(0, r)
            with pe.Fori(1, IT) as i:
                for r in range(UN):
                    step1(i, r)
            step1(IT, 0)


_INS = ["x", "src", "dst", "edge_weight", "L0_gnn_W1", "L0_gnn_b1", "L0_gnn_W2", "L0_gnn_b2", "L0_gnn_W3", "L0_gnn_b3",
        "L1_gnn_W", "L1_gnn_b"]


def kernel(**inputs):
    import numpy as np
    import concourse.bacc as bacc
    from concourse.bass_utils import run_bass_kernel_spmd

    nc = bacc.Bacc("TRN2", target_bir_lowering=False, num_devices=1)
    arrays, args = {}, []
    for name in _INS:
        a = np.ascontiguousarray(inputs[name])
        arrays[f"in_{name}_dram"] = a
        args.append(nc.dram_tensor(f"in_{name}_dram", a.shape, mybir.dt.from_np(a.dtype), kind="ExternalInput").ap())
    out = nc.dram_tensor("out_dram", (N, D), F32, kind="ExternalOutput").ap()
    gnn_kernel(nc, *args, out)
    r = run_bass_kernel_spmd(nc, [arrays], core_ids=[0])
    return r.results[0]["out_dram"]
```
